# Optimizing a Trainium2 kernel written in Bass

```python
import numpy as np
import jax
import jax.numpy as jnp

def _softmax(x, axis=-1):
    return jax.nn.softmax(x, axis=axis)

def _gelu(x):
    return jax.nn.gelu(x, approximate=True)

def _silu(x):
    return jax.nn.silu(x)

def _sigmoid(x):
    return jax.nn.sigmoid(x)

def _layernorm(x, axis=-1, eps=1e-05):
    m = jnp.mean(x, axis=axis, keepdims=True)
    v = jnp.var(x, axis=axis, keepdims=True)
    return (x - m) / jnp.sqrt(v + eps)

def _scatter_add(tgt, idx, src, axis=0):
    return tgt.at[idx].add(src)

def _segment_sum(src, seg, n):
    return jax.ops.segment_sum(src, seg, n)
kernel_name = 'mk_cond_resid_d4_seqx_r4_c58935'

def setup_inputs(seed: int=0):
    np.random.seed(seed)
    _w = jnp.asarray

    def _rec_inputs():
        import jax
        import jax.numpy as jnp
        _rk = jax.random.key(seed)
        x = -0.000125 + 0.9999 * jax.random.normal(jax.random.fold_in(_rk, 1), (128, 64, 256), jnp.float32)
        _lenS = 64 - jax.random.randint(jax.random.fold_in(_rk, 7), (128,), 0, max(1, 64 // 4) + 1, jnp.int32)
        _lenS2 = 64 - jax.random.randint(jax.random.fold_in(_rk, 8), (128,), 0, max(1, 64 // 4) + 1, jnp.int32)
        cond_1024 = -0.00493535 + 1.00056 * jax.random.normal(jax.random.fold_in(_rk, 11), (128, 256), jnp.float32)
        return (x, cond_1024)
    x, cond_1024 = _rec_inputs()

    def _L0_cond_setup():
        import jax, jax.numpy as jnp
        import numpy as np
        N, T, D, H = (64, 128, 256, 256)
        key = jax.random.key(seed)
        k1, k2, k3, k4 = jax.random.split(key, 4)
        x = jax.random.normal(k1, (N, T, D), dtype=jnp.float32)
        h0 = jax.random.normal(k2, (N, H), dtype=jnp.float32)
        Wx = jax.random.normal(k3, (D, H), dtype=jnp.float32) / np.sqrt(D)
        Wh = jax.random.normal(k4, (H, H), dtype=jnp.float32) / np.sqrt(H)
        b = jnp.zeros((H,), dtype=jnp.float32)
        return {'x': x, 'h0': h0, 'Wx': Wx, 'Wh': Wh, 'b': b}
    _L0_cond_all = _L0_cond_setup()
    _L0_cond_in = {k: v for k, v in _L0_cond_all.items() if k in ('Wx', 'Wh', 'b')}
    del _L0_cond_all

    def _L1_cond_setup():
        import jax, jax.numpy as jnp
        import numpy as np
        import math
        IN_F = 256
        OUT_F = 256
        B = 16
        L = 1024
        key = jax.random.key(seed)
        k1, k2, k3 = jax.random.split(key, 3)
        Efou = jax.random.normal(k1, (B, L, IN_F), dtype=jnp.float32)
        y = jax.random.normal(k2, (B, IN_F), dtype=jnp.float32)
        weight = jax.random.normal(k3, (1, OUT_F, IN_F, 1), dtype=jnp.float32)
        return {'Efou': Efou, 'y': y, 'weight': weight}
    _L1_cond_all = _L1_cond_setup()
    _L1_cond_in = {k: v for k, v in _L1_cond_all.items() if k in ('weight',)}
    del _L1_cond_all

    def _L2_cond_setup():
        import jax, jax.numpy as jnp
        import numpy as np
        INPUT_DIM = 256
        HIDDEN_DIM = 256
        CHUNK_SIZE = 4

        def _linear_params(key, fan_in, fan_out):
            kw, kb = jax.random.split(key)
            bound = 1.0 / np.sqrt(fan_in)
            W = jax.random.uniform(kw, (fan_in, fan_out), jnp.float32, -bound, bound)
            b = jax.random.uniform(kb, (fan_out,), jnp.float32, -bound, bound)
            return (W, b)

        def _gru_forward(x, h0, Wz, bz, Wr, br, Wh, bh, Wp, bp):
            B, T, D = x.shape
            t = jnp.arange(T)
            do_prop = ((t + 1) % CHUNK_SIZE == 0) & (t < T - 1)
            xs = jnp.transpose(x, (1, 0, 2))

            def step(h, inp):
                x_t, prop = inp
                comb = jnp.concatenate([x_t, h], axis=-1)
                z = jax.nn.sigmoid(comb @ Wz + bz)
                r = jax.nn.sigmoid(comb @ Wr + br)
                comb2 = jnp.concatenate([x_t, r * h], axis=-1)
                h_cand = jnp.tanh(comb2 @ Wh + bh)
                h_new = (1.0 - z) * h + z * h_cand
                h_next = jnp.where(prop, jnp.tanh(h_new @ Wp + bp), h_new)
                return (h_next, h_new)
            _, ys = jax.lax.scan(step, h0, (xs, do_prop))
            return jnp.transpose(ys, (1, 0, 2))
        key = jax.random.key(seed)
        ks = jax.random.split(key, 6)
        x = jax.random.normal(ks[0], (64, 128, INPUT_DIM), jnp.float32)
        h0 = jax.random.normal(ks[1], (64, HIDDEN_DIM), jnp.float32)
        Wz, bz = _linear_params(ks[2], INPUT_DIM + HIDDEN_DIM, HIDDEN_DIM)
        Wr, br = _linear_params(ks[3], INPUT_DIM + HIDDEN_DIM, HIDDEN_DIM)
        Wh, bh = _linear_params(ks[4], INPUT_DIM + HIDDEN_DIM, HIDDEN_DIM)
        Wp, bp = _linear_params(ks[5], HIDDEN_DIM, HIDDEN_DIM)
        return {'x': x, 'h0': h0, 'Wz': Wz, 'bz': bz, 'Wr': Wr, 'br': br, 'Wh': Wh, 'bh': bh, 'Wp': Wp, 'bp': bp}
    _L2_cond_all = _L2_cond_setup()
    _L2_cond_in = {k: v for k, v in _L2_cond_all.items() if k in ('Wz', 'bz', 'Wr', 'br', 'Wh', 'bh', 'Wp', 'bp')}
    del _L2_cond_all

    def _L3_cond_setup():
        import jax, jax.numpy as jnp
        import numpy as np
        INPUT_DIM = 256
        LATENT_DIM = 256
        key = jax.random.key(seed)
        ks = jax.random.split(key, 8)
        B, T = (64, 128)
        concat_dim = INPUT_DIM + LATENT_DIM
        s = lambda fan_in: 1.0 / np.sqrt(fan_in)
        return {'x': jax.random.normal(ks[0], (B, T, INPUT_DIM), dtype=jnp.float32), 'h0': jax.random.normal(ks[1], (B, LATENT_DIM), dtype=jnp.float32), 'w_W': jax.random.uniform(ks[2], (concat_dim, 2 * LATENT_DIM), jnp.float32, -s(concat_dim), s(concat_dim)), 'w_b': jax.random.uniform(ks[3], (2 * LATENT_DIM,), jnp.float32, -s(concat_dim), s(concat_dim)), 'wx_W': jax.random.uniform(ks[4], (INPUT_DIM, LATENT_DIM), jnp.float32, -s(INPUT_DIM), s(INPUT_DIM)), 'wx_b': jax.random.uniform(ks[5], (LATENT_DIM,), jnp.float32, -s(INPUT_DIM), s(INPUT_DIM)), 'wh_W': jax.random.uniform(ks[6], (LATENT_DIM, LATENT_DIM), jnp.float32, -s(LATENT_DIM), s(LATENT_DIM)), 'wh_b': jax.random.uniform(ks[7], (LATENT_DIM,), jnp.float32, -s(LATENT_DIM), s(LATENT_DIM))}
    _L3_cond_all = _L3_cond_setup()
    _L3_cond_in = {k: v for k, v in _L3_cond_all.items() if k in ('w_W', 'w_b', 'wx_W', 'wx_b', 'wh_W', 'wh_b')}
    del _L3_cond_all
    return {'x': x, 'cond_1024': cond_1024, 'L0_cond_Wx': _L0_cond_in['Wx'], 'L0_cond_Wh': _L0_cond_in['Wh'], 'L0_cond_b': _L0_cond_in['b'], 'L1_cond_weight': _L1_cond_in['weight'], 'L2_cond_Wz': _L2_cond_in['Wz'], 'L2_cond_bz': _L2_cond_in['bz'], 'L2_cond_Wr': _L2_cond_in['Wr'], 'L2_cond_br': _L2_cond_in['br'], 'L2_cond_Wh': _L2_cond_in['Wh'], 'L2_cond_bh': _L2_cond_in['bh'], 'L2_cond_Wp': _L2_cond_in['Wp'], 'L2_cond_bp': _L2_cond_in['bp'], 'L3_cond_w_W': _L3_cond_in['w_W'], 'L3_cond_w_b': _L3_cond_in['w_b'], 'L3_cond_wx_W': _L3_cond_in['wx_W'], 'L3_cond_wx_b': _L3_cond_in['wx_b'], 'L3_cond_wh_W': _L3_cond_in['wh_W'], 'L3_cond_wh_b': _L3_cond_in['wh_b']}

def reference(x, cond_1024, L0_cond_Wx, L0_cond_Wh, L0_cond_b, L1_cond_weight, L2_cond_Wz, L2_cond_bz, L2_cond_Wr, L2_cond_br, L2_cond_Wh, L2_cond_bh, L2_cond_Wp, L2_cond_bp, L3_cond_w_W, L3_cond_w_b, L3_cond_wx_W, L3_cond_wx_b, L3_cond_wh_W, L3_cond_wh_b):
    import jax
    import jax.numpy as jnp

    def _L0_cond_ref(x, h0, Wx, Wh, b):
        import jax, jax.numpy as jnp
        import numpy as np
        N, T, D, H = (64, 128, 256, 256)
        xW = jnp.einsum('ntd,dh->nth', x, Wx) + b
        xW_t = jnp.swapaxes(xW, 0, 1)

        def step(prev_h, xw):
            next_h = jnp.tanh(prev_h @ Wh + xw)
            return (next_h, next_h)
        _, h_t = jax.lax.scan(step, h0, xW_t)
        return jnp.swapaxes(h_t, 0, 1)

    def _L1_cond_ref(Efou, y, weight):
        import jax, jax.numpy as jnp
        import numpy as np
        import math
        IN_F = 256
        OUT_F = 256
        B = 16
        L = 1024
        b, img_size, in_f = Efou.shape
        out_f = weight.shape[1]
        scale = 1.0 / math.sqrt(in_f)
        w = scale * weight[:, :, :, 0] * y[:, None, :]
        dnorm = jax.lax.rsqrt(jnp.sum(w * w, axis=2, keepdims=True) + 1e-08)
        w = w * dnorm
        E = Efou.reshape(b, in_f, img_size)
        x = jnp.einsum('boi,bil->bol', w, E)
        return x.reshape(b, img_size, out_f)

    def _L2_cond_ref(x, h0, Wz, bz, Wr, br, Wh, bh, Wp, bp):
        import jax, jax.numpy as jnp
        import numpy as np
        INPUT_DIM = 256
        HIDDEN_DIM = 256
        CHUNK_SIZE = 4

        def _linear_params(key, fan_in, fan_out):
            kw, kb = jax.random.split(key)
            bound = 1.0 / np.sqrt(fan_in)
            W = jax.random.uniform(kw, (fan_in, fan_out), jnp.float32, -bound, bound)
            b = jax.random.uniform(kb, (fan_out,), jnp.float32, -bound, bound)
            return (W, b)

        def _gru_forward(x, h0, Wz, bz, Wr, br, Wh, bh, Wp, bp):
            B, T, D = x.shape
            t = jnp.arange(T)
            do_prop = ((t + 1) % CHUNK_SIZE == 0) & (t < T - 1)
            xs = jnp.transpose(x, (1, 0, 2))

            def step(h, inp):
                x_t, prop = inp
                comb = jnp.concatenate([x_t, h], axis=-1)
                z = jax.nn.sigmoid(comb @ Wz + bz)
                r = jax.nn.sigmoid(comb @ Wr + br)
                comb2 = jnp.concatenate([x_t, r * h], axis=-1)
                h_cand = jnp.tanh(comb2 @ Wh + bh)
                h_new = (1.0 - z) * h + z * h_cand
                h_next = jnp.where(prop, jnp.tanh(h_new @ Wp + bp), h_new)
                return (h_next, h_new)
            _, ys = jax.lax.scan(step, h0, (xs, do_prop))
            return jnp.transpose(ys, (1, 0, 2))
        return _gru_forward(x, h0, Wz, bz, Wr, br, Wh, bh, Wp, bp)

    def _L3_cond_ref(x, h0, w_W, w_b, wx_W, wx_b, wh_W, wh_b):
        import jax, jax.numpy as jnp
        import numpy as np
        INPUT_DIM = 256
        LATENT_DIM = 256
        xT = jnp.swapaxes(x, 0, 1)

        def step(h, x_t):
            fused = jax.nn.sigmoid(jnp.concatenate([x_t, h], axis=-1) @ w_W + w_b)
            hidden_state, output_state = jnp.split(fused, 2, axis=-1)
            memory_state = x_t @ wx_W + wx_b + hidden_state * (h @ wh_W + wh_b)
            h_new = output_state * h + (1.0 - output_state) * jnp.tanh(memory_state)
            return (h_new, h_new)
        _, hs = jax.lax.scan(step, h0, xT)
        return jnp.swapaxes(hs, 0, 1)
    x = x + _L0_cond_ref(x, cond_1024, L0_cond_Wx, L0_cond_Wh, L0_cond_b)
    x = x + _L1_cond_ref(x, cond_1024, L1_cond_weight)
    x = x + _L2_cond_ref(x, cond_1024, L2_cond_Wz, L2_cond_bz, L2_cond_Wr, L2_cond_br, L2_cond_Wh, L2_cond_bh, L2_cond_Wp, L2_cond_bp)
    x = x + _L3_cond_ref(x, cond_1024, L3_cond_w_W, L3_cond_w_b, L3_cond_wx_W, L3_cond_wx_b, L3_cond_wh_W, L3_cond_wh_b)
    return x

_drawn_inputs = setup_inputs


def setup_inputs(seed=0):
    import zlib

    import numpy as np

    out = dict(_drawn_inputs(seed))
    spreads = {'L0_cond_b': (0.0, 0.1)}
    factors = {'L2_cond_bz': 24.672,
     'L2_cond_Wr': 27.198,
     'L2_cond_br': 64.0,
     'L2_cond_bh': 6.067,
     'L2_cond_bp': 8.0,
     'L3_cond_w_b': 23.108,
     'L3_cond_wx_b': 4.381,
     'L3_cond_wh_b': 8.0}
    for name, (base, spread) in spreads.items():
        noise = np.random.default_rng([zlib.crc32(name.encode()), seed]).standard_normal(out[name].shape)
        drawn = base * np.exp(spread * noise) if base else spread * noise
        out[name] = jnp.asarray(drawn.astype(out[name].dtype))
    for name, factor in factors.items():
        out[name] = (out[name] * factor).astype(out[name].dtype)
    return out
```

```python
import concourse.bass as bass
from concourse import mybir
from concourse.alu_op_type import AluOpType as ALU
from contextlib import ExitStack

F32 = mybir.dt.float32
F16 = mybir.dt.float16
I32 = mybir.dt.int32
ACT = mybir.ActivationFunctionType
AX = mybir.AxisListType.X

P = 128
D = 256
KC = D // P
UNROLL = 4


class Count:

    def __init__(self, eng, first):
        self.eng, self.first, self.known = eng, first, {}

    def __call__(self, k):
        if isinstance(self.first, int):
            return self.first + k
        if k not in self.known:
            self.known[k] = self.eng.snap(self.first + k)
        return self.known[k]


def build_kernel(nc, a, out):
    B, T, _ = a["x"].shape
    L = T * D // D
    assert B == P and T % UNROLL == 0 and a["x"].shape[2] == D
    GROUPS = T // UNROLL

    W_EXP, A_EXP = 14, 9

    CW = KC * D
    Z0, R0, C0, G0, P0, MX0, MH0, CHUNKS = 0, 2, 4, 6, 10, 11, 12, 14
    XMAX, HMAX = CHUNKS, CHUNKS + 1
    SZ, SR, SC, SG, SP, SM, SA = range(7)
    NS = 7

    ctx = ExitStack()
    with ctx:
        def sb(name, shape, dt=F32):
            return ctx.enter_context(nc.sbuf_tensor(name, shape, dt))

        def sem(name):
            return ctx.enter_context(nc.semaphore(name))

        X = sb("X", [P, T * D])
        X_il = X[:, :].rearrange("p (i l) -> p i l", l=L)
        stage = sb("stage", [P, 2, D])
        xT = sb("xT", [P, 2, KC, B])
        ident = sb("ident", [P, P])
        ones = sb("ones", [P, D])
        cond = sb("cond", [P, D])
        condT = sb("condT", [P, KC, B])
        condT2 = sb("condT2", [P, KC, B])
        wx0 = sb("wx0", [P, KC, D])
        wh0 = sb("wh0", [P, KC, D])
        b0 = sb("b0", [P, KC])
        h0T = sb("h0T", [P, 2, KC, B])
        w1 = sb("w1", [P, KC, D])
        w1T = sb("w1T", [P, KC, D])
        w1T2 = sb("w1T2", [P, KC, D])
        norm_v = sb("norm_v", [P, D])
        norm_s = sb("norm_s", [P, D])
        norm_r = sb("norm_r", [P, D])
        norm_q = sb("norm_q", [P, D])
        gain = sb("gain", [P, D])
        ey = sb("ey", [P, 2, D])
        eyT = sb("eyT", [P, 2, KC, B])
        mod = sb("mod", [P, 2, D])
        W = sb("W", [P, CHUNKS * CW])
        W_hi = sb("W_hi", [P, CHUNKS * CW], F16)
        W_lo = sb("W_lo", [P, CHUNKS * CW], F16)
        bz = sb("bz", [P, KC])
        br = sb("br", [P, KC])
        bc = sb("bc", [P, KC])
        bp = sb("bp", [P, KC])
        bg = sb("bg", [P, 2 * KC])
        bx = sb("bx", [P, KC])
        bm = sb("bm", [P, KC])
        bm_s = sb("bm_s", [P, KC])
        xmax = sb("xmax", [P, T])
        peak = sb("peak", [P, CHUNKS + 2])
        peak_all = sb("peak_all", [P, CHUNKS + 2])
        top = sb("top", [P, NS])
        power = sb("power", [P, NS])
        scale = sb("scale", [P, NS])
        undo = sb("undo", [P, NS])
        undo_sum = sb("undo_sum", [P, NS])
        scale_m = sb("scale_m", [P, 1])
        chunk_scale = sb("chunk_scale", [P, CHUNKS])
        x2T = sb("x2T", [P, 2, KC * B])
        x2_hi = sb("x2_hi", [P, KC * B], F16)
        x2_lo = sb("x2_lo", [P, KC * B], F16)
        rT = sb("rT", [P, KC * B])
        zT = sb("zT", [P, KC * B])
        cT = sb("cT", [P, KC * B])
        rh = sb("rh", [P, KC * B])
        rh_hi = sb("rh_hi", [P, KC * B], F16)
        rh_lo = sb("rh_lo", [P, KC * B], F16)
        zh = sb("zh", [P, KC * B])
        keep = sb("keep", [P, KC * B])
        zc = sb("zc", [P, KC * B])
        h2 = sb("h2", [P, 2, KC * B])
        h2p = sb("h2p", [P, KC * B])
        pT = sb("pT", [P, KC * B])
        h2_hi = sb("h2_hi", [P, KC * B], F16)
        h2_lo = sb("h2_lo", [P, KC * B], F16)
        x3T = sb("x3T", [P, UNROLL, KC * B])
        x3_hi = sb("x3_hi", [P, KC * B], F16)
        x3_lo = sb("x3_lo", [P, KC * B], F16)
        hidT = sb("hidT", [P, KC * B])
        outT = sb("outT", [P, KC * B])
        one_o = sb("one_o", [P, KC * B])
        oh = sb("oh", [P, KC * B])
        mem_h = sb("mem_h", [P, KC * B])
        mem = sb("mem", [P, KC * B])
        mT = sb("mT", [P, KC * B])
        om = sb("om", [P, KC * B])
        h3 = sb("h3", [P, 2, KC * B])
        h3_hi = sb("h3_hi", [P, KC * B], F16)
        h3_lo = sb("h3_lo", [P, KC * B], F16)
        x4T = sb("x4T", [P, 2, KC * B])

        banks = [ctx.enter_context(nc.psum_tensor(f"bank{i}", [P, 512], F32)) for i in range(8)]
        pre = banks[0:2]
        tin = banks[2:4]
        tout = banks[4:6]
        setup_ps = banks[6:8]
        mod_ps = banks[4:6]
        R_ps, Z_ps, C_ps, HID_ps, OUT_ps, M_ps, XIN_ps, XOUT_ps = banks

        x_loaded = sem("x_loaded")
        small_loaded = sem("small_loaded")
        w1_loaded = sem("w1_loaded")
        weights_loaded = sem("weights_loaded")
        ident_zero = sem("ident_zero")
        ident_ready = sem("ident_ready")
        pad_ready = sem("pad_ready")
        ones_ready = sem("ones_ready")
        staged = sem("staged")
        x_transposed = sem("x_transposed")
        xT_ready = sem("xT_ready")
        cond_transposed = sem("cond_transposed")
        condT_ready = sem("condT_ready")
        rnn_sum = sem("rnn_sum")
        rnn_h = [sem(f"rnn_h{k}") for k in range(KC)]
        h_transposed = sem("h_transposed")
        x1_ready = sem("x1_ready")
        w1_transposed = sem("w1_transposed")
        w1T_ready = sem("w1T_ready")
        norm_sum = sem("norm_sum")
        norm_root = sem("norm_root")
        setup_step = sem("setup_step")
        peaks_ready = sem("peaks_ready")
        peaks_shared = sem("peaks_shared")
        scales_ready = sem("scales_ready")
        w_scaled = sem("w_scaled")
        w_hi_ready = sem("w_hi_ready")
        w_lo_ready = sem("w_lo_ready")
        ey_ready = sem("ey_ready")
        e_transposed = sem("e_transposed")
        eyT_ready = sem("eyT_ready")
        mod_sum = sem("mod_sum")
        mod_ready = sem("mod_ready")
        x2_nat = sem("x2_nat")
        staged2 = sem("staged2")
        x2_transposed = sem("x2_transposed")
        x2T_ready = sem("x2T_ready")
        x2_hi_ready = sem("x2_hi_ready")
        x2_split = sem("x2_split")
        r_sum = sem("r_sum")
        z_sum = sem("z_sum")
        c_sum = sem("c_sum")
        p_sum = sem("p_sum")
        r_ready = sem("r_ready")
        z_ready = sem("z_ready")
        c_ready = sem("c_ready")
        p_ready = sem("p_ready")
        rh_ready = sem("rh_ready")
        rh_hi_ready = sem("rh_hi_ready")
        rh_split = sem("rh_split")
        zh_ready = sem("zh_ready")
        keep_ready = sem("keep_ready")
        zc_ready = sem("zc_ready")
        h2_ready = sem("h2_ready")
        h2_hi_ready = sem("h2_hi_ready")
        h2_split_p = sem("h2_split_p")
        h2p_ready = sem("h2p_ready")
        h2_next = sem("h2_next")
        x3_ready = sem("x3_ready")
        x3_hi_ready = sem("x3_hi_ready")
        x3_split = sem("x3_split")
        hid_sum = sem("hid_sum")
        out_sum = sem("out_sum")
        mem_sum = sem("mem_sum")
        hid_ready = sem("hid_ready")
        out_ready = sem("out_ready")
        mem_h_ready = sem("mem_h_ready")
        mem_ready = sem("mem_ready")
        m_ready = sem("m_ready")
        oh_ready = sem("oh_ready")
        om_ready = sem("om_ready")
        h3_ready = sem("h3_ready")
        h3_hi_ready = sem("h3_hi_ready")
        h3_split = sem("h3_split")
        x4_ready = sem("x4_ready")
        x4_transposed = sem("x4_transposed")
        x4_nat = sem("x4_nat")
        stored = sem("stored")
        state_ready = sem("state_ready")

        def valid(t, off=0):
            return t is None or 0 <= t + off < T

        block = ctx.enter_context(nc.Block())

        @block.sync
        def _(sp):
            GC = UNROLL * D
            xv = a["x"].rearrange("b t d -> b (t d)")
            ov = out.rearrange("b t d -> b (t d)")
            sp.dma_start(X[:, 0:GC], xv[:, 0:GC]).then_inc(x_loaded, 16)
            with sp.Fori(1, GROUPS) as g:
                sp.wait_ge(x_loaded, g * 16)
                sp.dma_start(X[:, bass.ds(g * GC, GC)], xv[:, bass.ds(g * GC, GC)]).then_inc(x_loaded, 16)
            sp.wait_ge(x4_nat, UNROLL)
            sp.dma_start(ov[:, 0:GC], X[:, 0:GC]).then_inc(stored, 16)
            with sp.Fori(1, GROUPS) as g:
                sp.wait_ge(x4_nat, g * UNROLL + UNROLL)
                sp.dma_start(ov[:, bass.ds(g * GC, GC)], X[:, bass.ds(g * GC, GC)]).then_inc(stored, 16)
            sp.wait_ge(stored, 16 * GROUPS)

        @block.gpsimd
        def _(pool):
            pool.memset(ident[:, :], 0.0).then_inc(ident_zero, 1)
            pool.memset(W[:, (CHUNKS - 1) * CW:], 0.0).then_inc(pad_ready, 1)
            pool.memset(ones[:, :], 1.0).then_inc(ones_ready, 1)
            pool.wait_ge(ident_zero, 1)
            pool.affine_select(out=ident[:, :], in_=ident[:, :], compare_op=ALU.not_equal, fill=1.0,
                               base=0, pattern=[[-1, P]], channel_multiplier=1).then_inc(ident_ready, 1)

            def rnn(t, j, n, pos):
                if valid(t, 3):
                    s = (j + 3) % 2
                    if t is None or t + 3 >= 2:
                        pool.wait_ge(x_transposed, n(2))
                    if (j + 3) % UNROLL == 0:
                        if t is None:
                            pool.wait_ge(x_loaded, (pos + 3) * (16 // UNROLL) + 16)
                        else:
                            pool.wait_ge(x_loaded, 16 * ((t + 3) // UNROLL + 1))
                    pool.tensor_tensor(stage[:, s, :], X[:, bass.ds((pos + 3) * D, D)], ones[:, :],
                                       ALU.mult).then_inc(staged, 1)

            pool.wait_ge(ones_ready, 1)
            for t in range(-3, UNROLL):
                rnn(t, t % UNROLL, lambda k, t=t: t + k, t)
            with pool.Fori(1, GROUPS - 1) as i:
                base = Count(pool, i * UNROLL)
                for j in range(UNROLL):
                    rnn(None, j, lambda k, j=j: base(j + k), i * UNROLL + j)
            for t in range(T - UNROLL, T):
                rnn(t, t % UNROLL, lambda k, t=t: t + k, t)

            pool.wait_ge(peaks_ready, 1)
            pool.partition_all_reduce(peak_all[:, :], peak[:, :], P, bass.bass_isa.ReduceOp.max
                                      ).then_inc(peaks_shared, 1)

            def modulate(t, j, n, pos):
                if valid(t, 2):
                    if t is None or t >= 0:
                        pool.wait_ge(e_transposed, n(1))
                    pool.tensor_tensor(ey[:, j % 2, :], X_il[:, :, bass.ds(pos + 2, 1)], cond[:, :],
                                       ALU.mult).then_inc(ey_ready, 1)

            pool.wait_ge(x1_ready, T)
            pool.wait_ge(small_loaded, 64)
            for t in range(-2, UNROLL):
                modulate(t, t % UNROLL, lambda k, t=t: t + k, t)
            with pool.Fori(1, GROUPS - 1) as i:
                base = Count(pool, i * UNROLL)
                for j in range(UNROLL):
                    modulate(None, j, lambda k, j=j: base(j + k), i * UNROLL + j)
            for t in range(T - UNROLL, T):
                modulate(t, t % UNROLL, lambda k, t=t: t + k, t)

            def gates(t, j, n, pos):
                if valid(t, 2):
                    if t is None or t >= 0:
                        pool.wait_ge(x2_transposed, n(1))
                    pool.tensor_tensor(stage[:, j % 2, :], X[:, bass.ds((pos + 2) * D, D)], ones[:, :],
                                       ALU.mult).then_inc(staged2, 1)
                if valid(t, -2):
                    pool.wait_ge(out_ready, n(-1))
                    pool.tensor_tensor(oh[:, :], outT[:, :], h3[:, (j + 1) % 2, :], ALU.mult)
                    pool.tensor_scalar(one_o[:, :], outT[:, :], -1.0, 1.0, ALU.mult, ALU.add
                                       ).then_inc(oh_ready, 1)
                if valid(t):
                    h = h2p[:, :] if j == 0 and (t is None or t > 0) else h2[:, (j + 1) % 2, :]
                    pool.wait_ge(z_ready, n(1))
                    pool.tensor_tensor(zh[:, :], zT[:, :], h, ALU.mult).then_inc(zh_ready, 1)
                    pool.wait_ge(zh_ready, n(1))
                    pool.tensor_tensor(keep[:, :], h, zh[:, :], ALU.subtract).then_inc(keep_ready, 1)
                if valid(t, -2):
                    pool.wait_ge(h3_ready, n(-1))
                    if t is None or t >= 4:
                        pool.wait_ge(x4_transposed, n(-3))
                    pool.tensor_tensor(x4T[:, j % 2, :], x3T[:, (j + 2) % UNROLL, :], h3[:, j % 2, :],
                                       ALU.add).then_inc(x4_ready, 1)
                if valid(t):
                    pool.wait_ge(h2_ready, n(1))
                    pool.tensor_tensor(x3T[:, j, :], x2T[:, j % 2, :], h2[:, j % 2, :], ALU.add
                                       ).then_inc(x3_ready, 1)
                    pool.wait_ge(x3_hi_ready, n(1))
                    pool.tensor_tensor(x3_lo[:, :], x3T[:, j, :], x3_hi[:, :], ALU.subtract
                                       ).then_inc(x3_split, 1)

            pool.wait_ge(x2_nat, L)
            pool.wait_ge(state_ready, 1)
            for t in range(-2, UNROLL):
                gates(t, t % UNROLL, lambda k, t=t: t + k, t)
            with pool.Fori(1, GROUPS - 1) as i:
                base = Count(pool, i * UNROLL)
                for j in range(UNROLL):
                    gates(None, j, lambda k, j=j: base(j + k), i * UNROLL + j)
            for t in range(T - UNROLL, T + 4):
                gates(t, t % UNROLL, lambda k, t=t: t + k, t)

        @block.scalar
        def _(act):
            def cols(v, width):
                return v.rearrange("(c p) n -> p c n", p=P), width

            def bias(dst, src):
                act.dma_start(dst[:, :], src.rearrange("(c p) -> p c", p=P),
                              allow_slow_non_contiguous=True).then_inc(weights_loaded, 16)

            act.dma_start(wx0[:, :, :], a["L0_cond_Wx"].rearrange("(c p) n -> p c n", p=P)).then_inc(small_loaded, 16)
            act.dma_start(cond[:, :], a["cond_1024"]).then_inc(small_loaded, 16)
            act.dma_start(wh0[:, :, :], a["L0_cond_Wh"].rearrange("(c p) n -> p c n", p=P)).then_inc(small_loaded, 16)
            act.dma_start(b0[:, :], a["L0_cond_b"].rearrange("(c p) -> p c", p=P),
                          allow_slow_non_contiguous=True).then_inc(small_loaded, 16)
            act.dma_start(w1[:, :, :], a["L1_cond_weight"].rearrange("e (c p) i f -> p c (e i f)", p=P)
                          ).then_inc(w1_loaded, 16)
            for first, name, n in ((Z0, "L2_cond_Wz", 2), (R0, "L2_cond_Wr", 2), (C0, "L2_cond_Wh", 2),
                                   (G0, "L3_cond_w_W", 4), (P0, "L2_cond_Wp", 1), (MX0, "L3_cond_wx_W", 1),
                                   (MH0, "L3_cond_wh_W", 1)):
                src = a[name].rearrange("(c p) n -> p c n", p=P)
                act.dma_start(W[:, first * CW:(first + n) * CW].rearrange("p (c n) -> p c n", n=src.shape[2]),
                              src).then_inc(weights_loaded, 16)
            for dst, name in ((bz, "L2_cond_bz"), (br, "L2_cond_br"), (bc, "L2_cond_bh"), (bp, "L2_cond_bp"),
                              (bg, "L3_cond_w_b"), (bx, "L3_cond_wx_b"), (bm, "L3_cond_wh_b")):
                bias(dst, a[name])

            def rnn(t, j, n, pos):
                if valid(t):
                    act.wait_ge(rnn_sum, n(1))
                    for f in range(KC):
                        nc.scalar.activation(h0T[:, j % 2, f, :], pre[j % 2][:, f * B:(f + 1) * B], ACT.Tanh,
                                             bias=b0[:, f:f + 1]).then_inc(rnn_h[f], 1)

            act.wait_ge(small_loaded, 64)
            for t in range(UNROLL):
                rnn(t, t % UNROLL, lambda k, t=t: t + k, t)
            act.wait_ge(setup_step, 1)
            nc.scalar.activation(norm_s[:, :], norm_v[:, :], ACT.Sqrt).then_inc(norm_root, 1)
            with act.Fori(1, GROUPS - 1) as i:
                base = Count(act, i * UNROLL)
                for j in range(UNROLL):
                    rnn(None, j, lambda k, j=j: base(j + k), i * UNROLL + j)
            for t in range(T - UNROLL, T):
                rnn(t, t % UNROLL, lambda k, t=t: t + k, t)

            def modulate(t, j, n, pos):
                if valid(t, 2):
                    act.wait_ge(e_transposed, n(3))
                    nc.scalar.activation(eyT[:, j % 2, :, :].rearrange("p c b -> p (c b)"),
                                         tin[j % 2][:, 0:KC * B], ACT.Copy).then_inc(eyT_ready, 1)

            for t in range(-2, UNROLL):
                modulate(t, t % UNROLL, lambda k, t=t: t + k, t)
            act.wait_ge(scales_ready, 1)
            act.wait_ge(weights_loaded, 16 * 14)
            with act.Fori(1, GROUPS - 1) as i:
                base = Count(act, i * UNROLL)
                done = act.snap(i)
                for j in range(UNROLL):
                    modulate(None, j, lambda k, j=j: base(j + k), i * UNROLL + j)
                    chunk = W[:, bass.ds(i * CW - CW, CW)]
                    if j == 0:
                        nc.scalar.activation(chunk, chunk, ACT.Copy,
                                             scale=chunk_scale[:, bass.ds(i - 1, 1)]).then_inc(w_scaled, 1)
                    if j == 2:
                        act.wait_ge(w_scaled, done)
                        nc.scalar.activation(W_hi[:, bass.ds(i * CW - CW, CW)], chunk, ACT.Copy
                                             ).then_inc(w_hi_ready, 1)
            for t in range(T - UNROLL, T):
                modulate(t, t % UNROLL, lambda k, t=t: t + k, t)

            def gate(dst, src, func, column, b, ready):
                for f in range(KC):
                    last = nc.scalar.activation(dst[:, f * B:(f + 1) * B], src[:, f * B:(f + 1) * B], func,
                                                bias=b[:, f:f + 1], scale=undo_sum[:, column:column + 1])
                last.then_inc(ready, 1)

            def gates(t, j, n, pos):
                if valid(t):
                    act.wait_ge(r_sum, n(1))
                    gate(rT, R_ps, ACT.Sigmoid, SR, br, r_ready)
                if valid(t, -2):
                    act.wait_ge(mem_ready, n(-1))
                    gate(mT, mem, ACT.Tanh, SM, bx, m_ready)
                if valid(t):
                    act.wait_ge(z_sum, n(1))
                    gate(zT, Z_ps, ACT.Sigmoid, SZ, bz, z_ready)
                if valid(t, 1):
                    act.wait_ge(x2_transposed, n(2))
                    if t is None or t >= 1:
                        act.wait_ge(x3_ready, n(0))
                    nc.scalar.activation(x2T[:, (j + 1) % 2, :], XIN_ps[:, 0:KC * B], ACT.Copy,
                                         scale=scale[:, SA:SA + 1]).then_inc(x2T_ready, 1)
                if valid(t, -4):
                    act.wait_ge(x4_transposed, n(-3))
                    nc.scalar.activation(X[:, bass.ds((pos - 4) * D, D)], XOUT_ps[:, 0:D], ACT.Copy,
                                         scale=undo[:, SA:SA + 1]).then_inc(x4_nat, 1)
                if valid(t):
                    act.wait_ge(c_sum, n(1))
                    gate(cT, C_ps, ACT.Tanh, SC, bc, c_ready)
                if valid(t, -1):
                    act.wait_ge(hid_sum, n(0))
                    gate(hidT, HID_ps, ACT.Sigmoid, SG, bg, hid_ready)
                if valid(t) and j == UNROLL - 1 and (t is None or t < T - 1):
                    act.wait_ge(p_sum, (pos + 1) // UNROLL if t is not None else group(pos))
                    gate(pT, R_ps[:, KC * B:], ACT.Tanh, SP, bp, p_ready)
                if valid(t, -1):
                    act.wait_ge(out_sum, n(0))
                    gate(outT, OUT_ps, ACT.Sigmoid, SG, bg[:, KC:], out_ready)

            for t in range(-2, UNROLL):
                group = None
                gates(t, t % UNROLL, lambda k, t=t: t + k, t)
            with act.Fori(1, GROUPS - 1) as i:
                base = Count(act, i * UNROLL)
                nth = act.snap(i + 1)
                group = lambda pos: nth
                for j in range(UNROLL):
                    gates(None, j, lambda k, j=j: base(j + k), i * UNROLL + j)
            for t in range(T - UNROLL, T + 4):
                gates(t, t % UNROLL, lambda k, t=t: t + k, t)

        @block.vector
        def _(dve):
            dve.wait_ge(cond_transposed, 1)
            nc.vector.tensor_copy(condT[:, :, :].rearrange("p c b -> p (c b)"), setup_ps[0][:, 0:KC * B]
                                  ).then_inc(condT_ready, 1)

            def rnn(t, j, n, pos):
                if valid(t, 2):
                    dve.wait_ge(x_transposed, n(3))
                    nc.vector.tensor_copy(xT[:, j % 2, :, :].rearrange("p c b -> p (c b)"),
                                          tin[j % 2][:, 0:KC * B]).then_inc(xT_ready, 1)
                if valid(t, -1):
                    dve.wait_ge(h_transposed, n(0))
                    x1 = X[:, bass.ds((pos - 1) * D, D)]
                    nc.vector.tensor_tensor(x1, tout[(j + 1) % 2][:, 0:D], x1, ALU.add).then_inc(x1_ready, 1)
                if valid(t, -2):
                    dve.wait_ge(x1_ready, n(-1))
                    nc.vector.tensor_reduce(xmax[:, bass.ds(pos - 2, 1)], X[:, bass.ds((pos - 2) * D, D)],
                                            AX, ALU.max, apply_absolute_value=True)

            for t in range(-2, UNROLL):
                rnn(t, t % UNROLL, lambda k, t=t: t + k, t)

            chain = [0]

            def link(ins):
                chain[0] += 1
                ins.then_inc(setup_step, 1)
                dve.wait_ge(setup_step, chain[0])

            dve.wait_ge(w1_transposed, 1)
            nc.vector.tensor_copy(w1T[:, :, :].rearrange("p c o -> p (c o)"), setup_ps[1][:, 0:CW]
                                  ).then_inc(w1T_ready, 1)
            dve.wait_ge(w1T_ready, 1)
            nc.vector.tensor_tensor(w1T2[:, :, :].rearrange("p c o -> p (c o)"),
                                    w1T[:, :, :].rearrange("p c o -> p (c o)"),
                                    w1T[:, :, :].rearrange("p c o -> p (c o)"), ALU.mult)
            nc.vector.tensor_tensor(condT2[:, :, :].rearrange("p c b -> p (c b)"),
                                    condT[:, :, :].rearrange("p c b -> p (c b)"),
                                    condT[:, :, :].rearrange("p c b -> p (c b)"), ALU.mult
                                    ).then_inc(w1T_ready, 1)
            dve.wait_ge(norm_sum, 1)
            link(nc.vector.tensor_scalar(norm_v[:, :], setup_ps[0][:, 0:D], 1.0 / D, 1e-8, ALU.mult, ALU.add))
            dve.wait_ge(norm_root, 1)
            link(nc.vector.reciprocal(norm_r[:, :], norm_s[:, :]))
            link(nc.vector.tensor_tensor(norm_q[:, :], norm_r[:, :], norm_r[:, :], ALU.mult))
            link(nc.vector.tensor_tensor(norm_q[:, :], norm_q[:, :], norm_v[:, :], ALU.mult))
            link(nc.vector.tensor_scalar(norm_q[:, :], norm_q[:, :], -0.5, 1.5, ALU.mult, ALU.add))
            link(nc.vector.tensor_tensor(gain[:, :], norm_r[:, :], norm_q[:, :], ALU.mult))
            link(nc.vector.tensor_scalar(gain[:, :], gain[:, :], float(D) ** -0.5, None, ALU.mult))

            dve.wait_ge(weights_loaded, 16 * 14)
            dve.wait_ge(pad_ready, 1)
            with dve.Fori(1, GROUPS - 1) as i:
                base = Count(dve, i * UNROLL)
                for j in range(UNROLL):
                    rnn(None, j, lambda k, j=j: base(j + k), i * UNROLL + j)
                nc.vector.tensor_reduce(peak[:, bass.ds(i - 1, 1)], W[:, bass.ds(i * CW - CW, CW)], AX, ALU.max,
                                        apply_absolute_value=True)
            for t in range(T - UNROLL, T + 2):
                rnn(t, t % UNROLL, lambda k, t=t: t + k, t)

            link(nc.vector.tensor_reduce(peak[:, HMAX:HMAX + 1], cond[:, :], AX, ALU.max,
                                         apply_absolute_value=True))
            nc.vector.tensor_reduce(peak[:, XMAX:XMAX + 1], xmax[:, :], AX, ALU.max).then_inc(peaks_ready, 1)
            dve.wait_ge(peaks_shared, 1)
            pk = peak_all

            def widest(column, first, count):
                return nc.vector.tensor_reduce(top[:, column:column + 1], pk[:, first:first + count], AX, ALU.max)

            widest(SZ, Z0, 2)
            widest(SR, R0, 2)
            widest(SC, C0, 2)
            widest(SG, G0, 4)
            widest(SP, P0, 1)
            widest(SM, MX0, 2)
            link(widest(SA, XMAX, 2))
            nc.vector.tensor_scalar(top[:, 0:SA], top[:, 0:SA], 2.0 ** -100, None, ALU.max)
            link(nc.vector.tensor_scalar(top[:, SA:NS], top[:, SA:NS], 1.0, None, ALU.max))
            link(nc.vector.tensor_scalar(power[:, :].bitcast(I32), top[:, :].bitcast(I32), 0x7F800000, None,
                                         ALU.bitwise_and))
            for lo_, hi_, e in ((0, SA, W_EXP), (SA, NS, A_EXP)):
                nc.vector.tensor_scalar(scale[:, lo_:hi_].bitcast(I32), power[:, lo_:hi_].bitcast(I32), -1.0,
                                        float((254 + e) << 23), ALU.mult, ALU.add)
                last = nc.vector.tensor_scalar(undo[:, lo_:hi_], power[:, lo_:hi_], 2.0 ** -e, None, ALU.mult)
            link(last)
            for c0, n, s in ((Z0, 2, SZ), (R0, 2, SR), (C0, 2, SC), (G0, 4, SG), (P0, 1, SP), (MX0, 3, SM)):
                nc.vector.tensor_copy(chunk_scale[:, c0:c0 + n], scale[:, s:s + 1].to_broadcast([P, n]))
            nc.vector.tensor_scalar(undo_sum[:, :], undo[:, :], undo[:, SA:SA + 1], None, ALU.mult)
            link(nc.vector.tensor_scalar(scale_m[:, :], scale[:, SM:SM + 1], scale[:, SA:SA + 1], None, ALU.mult))
            nc.vector.tensor_scalar(bm_s[:, :], bm[:, :], scale_m[:, :], None, ALU.mult).then_inc(scales_ready, 1)

            def modulate(t, j, n, pos):
                if valid(t):
                    dve.wait_ge(mod_sum, n(1))
                    if t is None or t >= 2:
                        dve.wait_ge(x2_nat, n(-1))
                    nc.vector.tensor_tensor(mod[:, j % 2, :], mod_ps[j % 2][:, 0:D], gain[:, :], ALU.mult
                                            ).then_inc(mod_ready, 1)
                if valid(t, -1):
                    dve.wait_ge(mod_ready, n(0))
                    x2 = X_il[:, :, bass.ds(pos - 1, 1)]
                    nc.vector.tensor_tensor(x2, mod[:, (j + 1) % 2, :], x2, ALU.add).then_inc(x2_nat, 1)

            for t in range(UNROLL):
                modulate(t, t % UNROLL, lambda k, t=t: t + k, t)
            with dve.Fori(1, GROUPS - 1) as i:
                base = Count(dve, i * UNROLL)
                chunks = dve.snap(i)
                for j in range(UNROLL):
                    modulate(None, j, lambda k, j=j: base(j + k), i * UNROLL + j)
                dve.wait_ge(w_hi_ready, chunks)
                nc.vector.tensor_tensor(W_lo[:, bass.ds(i * CW - CW, CW)], W[:, bass.ds(i * CW - CW, CW)],
                                        W_hi[:, bass.ds(i * CW - CW, CW)], ALU.subtract).then_inc(w_lo_ready, 1)
            for dst in (h2, h3):
                last = nc.vector.tensor_scalar(dst[:, 1, :], condT[:, :, :].rearrange("p c b -> p (c b)"),
                                               scale[:, SA:SA + 1], None, ALU.mult)
            link(last)
            nc.vector.tensor_copy(h2_hi[:, :], h2[:, 1, :])
            link(nc.vector.tensor_copy(h3_hi[:, :], h3[:, 1, :]))
            nc.vector.tensor_tensor(h2_lo[:, :], h2[:, 1, :], h2_hi[:, :], ALU.subtract).then_inc(h2_next, 1)
            nc.vector.tensor_tensor(h3_lo[:, :], h3[:, 1, :], h3_hi[:, :], ALU.subtract).then_inc(h3_split, 1)
            link(nc.vector.memset(h2p[:, :], 0.0))
            nc.vector.memset(zc[:, :], 0.0).then_inc(state_ready, 1)
            for t in range(T - UNROLL, T + 1):
                modulate(t, t % UNROLL, lambda k, t=t: t + k, t)

            def gates(t, j, n, pos):
                if valid(t):
                    h = h2p[:, :] if j == 0 and (t is None or t > 0) else h2[:, (j + 1) % 2, :]
                    dve.wait_ge(r_ready, n(1))
                    nc.vector.tensor_tensor(rh[:, :], rT[:, :], h, ALU.mult).then_inc(rh_ready, 1)
                    dve.wait_ge(rh_ready, n(1))
                    nc.vector.tensor_copy(rh_hi[:, :], rh[:, :]).then_inc(rh_hi_ready, 1)
                    dve.wait_ge(rh_hi_ready, n(1))
                    nc.vector.tensor_tensor(rh_lo[:, :], rh[:, :], rh_hi[:, :], ALU.subtract
                                            ).then_inc(rh_split, 1)
                if valid(t, -2):
                    dve.wait_ge(m_ready, n(-1))
                    dve.wait_ge(oh_ready, n(-1))
                    nc.vector.scalar_tensor_tensor(om[:, :], mT[:, :], scale[:, SA:SA + 1], one_o[:, :],
                                                   ALU.mult, ALU.mult).then_inc(om_ready, 1)
                if valid(t, 1):
                    dve.wait_ge(x2T_ready, n(2))
                    if t is None or t >= 0:
                        dve.wait_ge(r_sum, n(1))
                    nc.vector.tensor_copy(x2_hi[:, :], x2T[:, (j + 1) % 2, :]).then_inc(x2_hi_ready, 1)
                if valid(t, -2):
                    dve.wait_ge(om_ready, n(-1))
                    nc.vector.tensor_tensor(h3[:, j % 2, :], om[:, :], oh[:, :], ALU.add).then_inc(h3_ready, 1)
                if valid(t, 1):
                    dve.wait_ge(x2_hi_ready, n(2))
                    nc.vector.tensor_tensor(x2_lo[:, :], x2T[:, (j + 1) % 2, :], x2_hi[:, :], ALU.subtract
                                            ).then_inc(x2_split, 1)
                if valid(t, -2):
                    dve.wait_ge(h3_ready, n(-1))
                    nc.vector.tensor_copy(h3_hi[:, :], h3[:, j % 2, :]).then_inc(h3_hi_ready, 1)
                    dve.wait_ge(h3_hi_ready, n(-1))
                    nc.vector.tensor_tensor(h3_lo[:, :], h3[:, j % 2, :], h3_hi[:, :], ALU.subtract
                                            ).then_inc(h3_split, 1)
                if valid(t):
                    dve.wait_ge(c_ready, n(1))
                    nc.vector.scalar_tensor_tensor(zc[:, :], cT[:, :], scale[:, SA:SA + 1], zT[:, :],
                                                   ALU.mult, ALU.mult).then_inc(zc_ready, 1)
                    dve.wait_ge(keep_ready, n(1))
                    dve.wait_ge(zc_ready, n(1))
                    nc.vector.tensor_tensor(h2[:, j % 2, :], zc[:, :], keep[:, :], ALU.add).then_inc(h2_ready, 1)
                    if t is None or t < T - 1:
                        dve.wait_ge(h2_ready, n(1))
                        nc.vector.tensor_copy(h2_hi[:, :], h2[:, j % 2, :]).then_inc(h2_hi_ready, 1)
                        dve.wait_ge(h2_hi_ready, pairs(t, j, pos))
                        nc.vector.tensor_tensor(h2_lo[:, :], h2[:, j % 2, :], h2_hi[:, :], ALU.subtract
                                                ).then_inc(h2_split_p if j == UNROLL - 1 else h2_next, 1)
                if valid(t) and j == UNROLL - 1 and (t is None or t < T - 1):
                    dve.wait_ge(p_ready, nth(t, pos))
                    nc.vector.tensor_scalar(h2p[:, :], pT[:, :], scale[:, SA:SA + 1], None, ALU.mult
                                            ).then_inc(h2p_ready, 1)
                    dve.wait_ge(h2p_ready, nth(t, pos))
                    nc.vector.tensor_copy(h2_hi[:, :], h2p[:, :]).then_inc(h2_hi_ready, 1)
                    dve.wait_ge(h2_hi_ready, pairs(t, j, pos, 1))
                    nc.vector.tensor_tensor(h2_lo[:, :], h2p[:, :], h2_hi[:, :], ALU.subtract
                                            ).then_inc(h2_next, 1)
                if valid(t):
                    dve.wait_ge(x3_ready, n(1))
                    nc.vector.tensor_copy(x3_hi[:, :], x3T[:, j, :]).then_inc(x3_hi_ready, 1)
                if valid(t, -1):
                    dve.wait_ge(mem_sum, n(0))
                    dve.wait_ge(hid_ready, n(0))
                    for f in range(KC):
                        at = slice(f * B, (f + 1) * B)
                        last = nc.vector.scalar_tensor_tensor(mem_h[:, at], M_ps[:, KC * B + f * B:KC * B + (f + 1) * B],
                                                              bm_s[:, f:f + 1], hidT[:, at], ALU.add, ALU.mult)
                    last.then_inc(mem_h_ready, 1)
                    dve.wait_ge(mem_h_ready, n(0))
                    nc.vector.tensor_tensor(mem[:, :], M_ps[:, 0:KC * B], mem_h[:, :], ALU.add
                                            ).then_inc(mem_ready, 1)

            known = {}

            def nth(t, pos):
                return (t + 1) // UNROLL if t is not None else known["nth"]

            def pairs(t, j, pos, more=0):
                if t is not None:
                    return t // UNROLL * (UNROLL + 1) + j + 1 + more
                if j + more not in known:
                    known[j + more] = dve.snap(known["i"] * (UNROLL + 1) + (j + more + 1))
                return known[j + more]

            for t in range(-2, UNROLL):
                gates(t, t % UNROLL, lambda k, t=t: t + k, t)
            with dve.Fori(1, GROUPS - 1) as i:
                base = Count(dve, i * UNROLL)
                known.clear()
                known["i"] = i
                known["nth"] = dve.snap(i + 1)
                for j in range(UNROLL):
                    gates(None, j, lambda k, j=j: base(j + k), i * UNROLL + j)
            for t in range(T - UNROLL, T + 4):
                gates(t, t % UNROLL, lambda k, t=t: t + k, t)

        @block.tensor
        def _(pe):
            def mm(dst, lhsT, rhs, start=False):
                return nc.tensor.matmul(dst, lhsT, rhs, start=start, stop=True, skip_group_check=True)

            def transposed(dst, src):
                for c in range(KC):
                    last = nc.tensor.transpose(dst[:, c * P:(c + 1) * P], src[:, c * P:(c + 1) * P], ident[:, :])
                return last

            pe.wait_ge(ident_ready, 1)
            pe.wait_ge(small_loaded, 64)
            transposed(setup_ps[0], cond).then_inc(cond_transposed, 1)

            def rnn(t, j, n, pos):
                if valid(t):
                    for k in range(KC):
                        if t == 0:
                            pe.wait_ge(condT_ready, 1)
                            h = condT[:, k, :]
                        else:
                            pe.wait_ge(rnn_h[k], n(0))
                            h = h0T[:, (j + 1) % 2, k, :]
                        for f in range(KC):
                            last = mm(pre[j % 2][:, f * B:(f + 1) * B], wh0[:, k, f * P:(f + 1) * P], h)
                    last.then_inc(rnn_sum, 1)
                if valid(t, 1):
                    pe.wait_ge(xT_ready, n(2))
                    for k in range(KC):
                        for f in range(KC):
                            mm(pre[(j + 1) % 2][:, f * B:(f + 1) * B], wx0[:, k, f * P:(f + 1) * P],
                               xT[:, (j + 1) % 2, k, :], start=(k == 0 and f == 0))
                if valid(t, 2):
                    pe.wait_ge(staged, n(3))
                    if t is None or t >= 0:
                        pe.wait_ge(xT_ready, n(1))
                    transposed(tin[j % 2], stage[:, j % 2, :]).then_inc(x_transposed, 1)
                if valid(t, -1):
                    if t == T:
                        for k in range(KC):
                            pe.wait_ge(rnn_h[k], T)
                    if t is None or t >= 3:
                        pe.wait_ge(x1_ready, n(-2))
                    transposed(tout[(j + 1) % 2], h0T[:, (j + 1) % 2, :, :].rearrange("p c b -> p (c b)")
                               ).then_inc(h_transposed, 1)

            for t in range(-2, UNROLL):
                rnn(t, t % UNROLL, lambda k, t=t: t + k, t)

            pe.wait_ge(w1_loaded, 16)
            for c in range(KC):
                for o in range(KC):
                    last = nc.tensor.transpose(setup_ps[1][:, c * D + o * P:c * D + (o + 1) * P],
                                               w1[:, o, c * P:(c + 1) * P], ident[:, :])
            last.then_inc(w1_transposed, 1)
            pe.wait_ge(w1T_ready, 2)
            for k in range(KC):
                last = mm(setup_ps[0][:, 0:D], condT2[:, k, :], w1T2[:, k, :], start=(k == 0))
            last.then_inc(norm_sum, 1)

            with pe.Fori(1, GROUPS - 1) as i:
                base = Count(pe, i * UNROLL)
                for j in range(UNROLL):
                    rnn(None, j, lambda k, j=j: base(j + k), i * UNROLL + j)
            for t in range(T - UNROLL, T + 1):
                rnn(t, t % UNROLL, lambda k, t=t: t + k, t)

            def modulate(t, j, n, pos):
                if valid(t):
                    pe.wait_ge(eyT_ready, n(1))
                    if t is None or t >= 2:
                        pe.wait_ge(mod_ready, n(-1))
                    for k in range(KC):
                        last = mm(mod_ps[j % 2][:, 0:D], eyT[:, j % 2, k, :], w1T[:, k, :], start=(k == 0))
                    last.then_inc(mod_sum, 1)
                if valid(t, 2):
                    pe.wait_ge(ey_ready, n(3))
                    if t is None or t >= 0:
                        pe.wait_ge(eyT_ready, n(1))
                    transposed(tin[j % 2], ey[:, j % 2, :]).then_inc(e_transposed, 1)

            for t in range(-2, UNROLL):
                modulate(t, t % UNROLL, lambda k, t=t: t + k, t)
            with pe.Fori(1, GROUPS - 1) as i:
                base = Count(pe, i * UNROLL)
                for j in range(UNROLL):
                    modulate(None, j, lambda k, j=j: base(j + k), i * UNROLL + j)
            for t in range(T - UNROLL, T):
                modulate(t, t % UNROLL, lambda k, t=t: t + k, t)

            def product(dst, w_at, x_hi, x_lo, begins=False):
                first = begins
                for k in range(KC):
                    for f in range(KC):
                        c = w_at(k, f)
                        for w in (W_hi, W_lo):
                            mm(dst[:, f * B:(f + 1) * B], w[:, c:c + P], x_hi[:, k * B:(k + 1) * B], first)
                            first = False
                for k in range(KC):
                    for f in range(KC):
                        c = w_at(k, f)
                        last = mm(dst[:, f * B:(f + 1) * B], W_hi[:, c:c + P], x_lo[:, k * B:(k + 1) * B])
                return last

            def block_at(chunk):
                return lambda k, f: chunk * CW + k * D + f * P

            def fused_at(half, part):
                return lambda k, f: (G0 + 2 * half + k) * CW + part * D + f * P

            def gates(t, j, n, pos):
                if valid(t):
                    pe.wait_ge(h2_next, n(1))
                    product(R_ps, block_at(R0 + 1), h2_hi, h2_lo).then_inc(r_sum, 1)
                    product(Z_ps, block_at(Z0 + 1), h2_hi, h2_lo).then_inc(z_sum, 1)
                if valid(t, -1):
                    pe.wait_ge(x3_split, n(0))
                    if t is None or t >= 2:
                        pe.wait_ge(mem_ready, n(-1))
                    product(M_ps, block_at(MX0), x3_hi, x3_lo, True)
                    if t is None or t >= 2:
                        pe.wait_ge(hid_ready, n(-1))
                    product(HID_ps, fused_at(0, 0), x3_hi, x3_lo, True)
                    if t is None or t >= 2:
                        pe.wait_ge(out_ready, n(-1))
                    product(OUT_ps, fused_at(0, 1), x3_hi, x3_lo, True)
                if valid(t):
                    pe.wait_ge(rh_split, n(1))
                    product(C_ps, block_at(C0 + 1), rh_hi, rh_lo).then_inc(c_sum, 1)
                if valid(t, -1):
                    pe.wait_ge(h3_split, n(0))
                    product(HID_ps, fused_at(1, 0), h3_hi, h3_lo).then_inc(hid_sum, 1)
                    product(M_ps[:, KC * B:], block_at(MH0), h3_hi, h3_lo).then_inc(mem_sum, 1)
                    product(OUT_ps, fused_at(1, 1), h3_hi, h3_lo).then_inc(out_sum, 1)
                if valid(t, 2):
                    pe.wait_ge(staged2, n(3))
                    if t is None or t >= -1:
                        pe.wait_ge(x2T_ready, n(2))
                    transposed(XIN_ps, stage[:, j % 2, :]).then_inc(x2_transposed, 1)
                if valid(t, -3):
                    pe.wait_ge(x4_ready, n(-2))
                    if t is None or t >= 4:
                        pe.wait_ge(x4_nat, n(-3))
                    transposed(XOUT_ps, x4T[:, (j + 1) % 2, :]).then_inc(x4_transposed, 1)
                if valid(t) and j == UNROLL - 1 and (t is None or t < T - 1):
                    pe.wait_ge(h2_split_p, nth(t))
                    product(R_ps[:, KC * B:], block_at(P0), h2_hi, h2_lo, True).then_inc(p_sum, 1)
                if valid(t, 1):
                    pe.wait_ge(x2_split, n(2))
                    if t is None or t >= 0:
                        pe.wait_ge(z_ready, n(1))
                    product(Z_ps, block_at(Z0), x2_hi, x2_lo, True)
                    if t is None or t >= 0:
                        pe.wait_ge(c_ready, n(1))
                    product(C_ps, block_at(C0), x2_hi, x2_lo, True)
                    if t is None or t >= 0:
                        pe.wait_ge(r_ready, n(1))
                    if j == UNROLL - 1 and (t is None or t >= 0):
                        pe.wait_ge(p_ready, nth(t))
                    product(R_ps, block_at(R0), x2_hi, x2_lo, True)

            known = {}

            def nth(t):
                return (t + 1) // UNROLL if t is not None else known["nth"]

            pe.wait_ge(w_lo_ready, CHUNKS)
            pe.wait_ge(mod_ready, L)
            for t in range(-2, UNROLL):
                gates(t, t % UNROLL, lambda k, t=t: t + k, t)
            with pe.Fori(1, GROUPS - 1) as i:
                base = Count(pe, i * UNROLL)
                known["nth"] = pe.snap(i + 1)
                for j in range(UNROLL):
                    gates(None, j, lambda k, j=j: base(j + k), i * UNROLL + j)
            for t in range(T - UNROLL, T + 4):
                gates(t, t % UNROLL, lambda k, t=t: t + k, t)


_INS = ["x", "cond_1024", "L0_cond_Wx", "L0_cond_Wh", "L0_cond_b", "L1_cond_weight", "L2_cond_Wz", "L2_cond_bz",
        "L2_cond_Wr", "L2_cond_br", "L2_cond_Wh", "L2_cond_bh", "L2_cond_Wp", "L2_cond_bp", "L3_cond_w_W",
        "L3_cond_w_b", "L3_cond_wx_W", "L3_cond_wx_b", "L3_cond_wh_W", "L3_cond_wh_b"]


def kernel(**inputs):
    import numpy as np
    import concourse.bacc as bacc
    from concourse.bass_utils import run_bass_kernel_spmd

    nc = bacc.Bacc("TRN2", target_bir_lowering=False, num_devices=1)
    arrays, aps = {}, {}
    for name in _INS:
        arr = np.ascontiguousarray(inputs[name])
        arrays[f"in_{name}"] = arr
        aps[name] = nc.dram_tensor(f"in_{name}", arr.shape, mybir.dt.from_np(arr.dtype), kind="ExternalInput").ap()
    out = nc.dram_tensor("out_x", arrays["in_x"].shape, F32, kind="ExternalOutput").ap()
    build_kernel(nc, aps, out)
    r = run_bass_kernel_spmd(nc, [arrays], core_ids=[0])
    return r.results[0]["out_x"]
```

```python
import concourse.bass as bass
from concourse import mybir
from concourse.alu_op_type import AluOpType as ALU
from contextlib import ExitStack

F32 = mybir.dt.float32
F16 = mybir.dt.float16
I32 = mybir.dt.int32
ACT = mybir.ActivationFunctionType
AX = mybir.AxisListType.X

P = 128
D = 256
KC = D // P
UNROLL = 4


class Count:

    def __init__(self, eng, first):
        self.eng, self.first, self.known = eng, first, {}

    def __call__(self, k):
        if isinstance(self.first, int):
            return self.first + k
        if k not in self.known:
            self.known[k] = self.eng.snap(self.first + k)
        return self.known[k]


def build_kernel(nc, a, out):
    B, T, _ = a["x"].shape
    L = T * D // D
    assert B == P and T % UNROLL == 0 and a["x"].shape[2] == D
    GROUPS = T // UNROLL

    W_EXP, A_EXP = 14, 9

    CW = KC * D
    Z0, R0, C0, G0, P0, MX0, MH0, CHUNKS = 0, 2, 4, 6, 10, 11, 12, 14
    XMAX, HMAX = CHUNKS, CHUNKS + 1
    SZ, SR, SC, SG, SP, SM, SA = range(7)
    NS = 7

    ctx = ExitStack()
    with ctx:
        def sb(name, shape, dt=F32):
            return ctx.enter_context(nc.sbuf_tensor(name, shape, dt))

        def sem(name):
            return ctx.enter_context(nc.semaphore(name))

        X = sb("X", [P, T * D])
        X_il = X[:, :].rearrange("p (i l) -> p i l", l=L)
        stage = sb("stage", [P, 2, D])
        xT = sb("xT", [P, 2, KC, B])
        ident = sb("ident", [P, P])
        ones = sb("ones", [P, D])
        warm = sb("warm", [P, 1])
        cond = sb("cond", [P, D])
        condT = sb("condT", [P, KC, B])
        condT2 = sb("condT2", [P, KC, B])
        wx0 = sb("wx0", [P, KC, D])
        wh0 = sb("wh0", [P, KC, D])
        b0 = sb("b0", [P, KC])
        h0T = sb("h0T", [P, 2, KC, B])
        w1 = sb("w1", [P, KC, D])
        w1T = sb("w1T", [P, KC, D])
        w1T2 = sb("w1T2", [P, KC, D])
        norm_v = sb("norm_v", [P, D])
        norm_r = sb("norm_r", [P, D])
        norm_q = sb("norm_q", [P, D])
        gain = sb("gain", [P, D])
        ey = sb("ey", [P, 2, D])
        eyT = sb("eyT", [P, 2, KC, B])
        mod = sb("mod", [P, 2, D])
        W = sb("W", [P, CHUNKS * CW])
        W_hi = sb("W_hi", [P, CHUNKS * CW], F16)
        W_lo = sb("W_lo", [P, CHUNKS * CW], F16)
        bz = sb("bz", [P, KC])
        br = sb("br", [P, KC])
        bc = sb("bc", [P, KC])
        bp = sb("bp", [P, KC])
        bg = sb("bg", [P, 2 * KC])
        bx = sb("bx", [P, KC])
        bm = sb("bm", [P, KC])
        bm_s = sb("bm_s", [P, KC])
        xmax = sb("xmax", [P, T])
        peak = sb("peak", [P, CHUNKS + 2])
        peak_all = sb("peak_all", [P, CHUNKS + 2])
        top = sb("top", [P, NS])
        power = sb("power", [P, NS])
        scale = sb("scale", [P, NS])
        undo = sb("undo", [P, NS])
        undo_sum = sb("undo_sum", [P, NS])
        scale_m = sb("scale_m", [P, 1])
        chunk_scale = sb("chunk_scale", [P, CHUNKS])
        x2T = sb("x2T", [P, 2, KC * B])
        x2_hi = sb("x2_hi", [P, KC * B], F16)
        x2_lo = sb("x2_lo", [P, KC * B], F16)
        rT = sb("rT", [P, KC * B])
        zT = sb("zT", [P, KC * B])
        cT = sb("cT", [P, KC * B])
        rh = sb("rh", [P, KC * B])
        rh_hi = sb("rh_hi", [P, KC * B], F16)
        rh_lo = sb("rh_lo", [P, KC * B], F16)
        zh = sb("zh", [P, KC * B])
        keep = sb("keep", [P, KC * B])
        zc = sb("zc", [P, KC * B])
        h2 = sb("h2", [P, 2, KC * B])
        h2p = sb("h2p", [P, KC * B])
        pT = sb("pT", [P, KC * B])
        h2_hi = sb("h2_hi", [P, KC * B], F16)
        h2_lo = sb("h2_lo", [P, KC * B], F16)
        x3T = sb("x3T", [P, UNROLL, KC * B])
        x3_hi = sb("x3_hi", [P, KC * B], F16)
        x3_lo = sb("x3_lo", [P, KC * B], F16)
        hidT = sb("hidT", [P, KC * B])
        outT = sb("outT", [P, KC * B])
        one_o = sb("one_o", [P, KC * B])
        oh = sb("oh", [P, KC * B])
        mem_h = sb("mem_h", [P, KC * B])
        mem = sb("mem", [P, KC * B])
        mT = sb("mT", [P, KC * B])
        om = sb("om", [P, KC * B])
        h3 = sb("h3", [P, 2, KC * B])
        h3_hi = sb("h3_hi", [P, KC * B], F16)
        h3_lo = sb("h3_lo", [P, KC * B], F16)
        x4T = sb("x4T", [P, 2, KC * B])

        banks = [ctx.enter_context(nc.psum_tensor(f"bank{i}", [P, 512], F32)) for i in range(8)]
        pre = banks[0:2]
        tin = banks[2:4]
        tout = banks[4:6]
        setup_ps = banks[6:8]
        mod_ps = banks[4:6]
        R_ps, Z_ps, C_ps, HID_ps, OUT_ps, M_ps, XIN_ps, XOUT_ps = banks
        P_ps = XIN_ps[:, KC * B:]

        x_loaded = sem("x_loaded")
        wx_loaded = sem("wx_loaded")
        cond_loaded = sem("cond_loaded")
        wh_loaded = sem("wh_loaded")
        b0_loaded = sem("b0_loaded")
        w1_loaded = sem("w1_loaded")
        weights_loaded = sem("weights_loaded")
        ident_zero = sem("ident_zero")
        ident_ready = sem("ident_ready")
        pad_ready = sem("pad_ready")
        ones_ready = sem("ones_ready")
        staged = sem("staged")
        x_transposed = sem("x_transposed")
        xT_ready = sem("xT_ready")
        cond_transposed = sem("cond_transposed")
        condT_ready = sem("condT_ready")
        rnn_sum = sem("rnn_sum")
        rnn_h = [sem(f"rnn_h{k}") for k in range(KC)]
        h_transposed = sem("h_transposed")
        x1_ready = sem("x1_ready")
        xmax_ready = sem("xmax_ready")
        w1_transposed = sem("w1_transposed")
        w1T_ready = sem("w1T_ready")
        norm_sum = sem("norm_sum")
        setup_step = sem("setup_step")
        peaks_ready = sem("peaks_ready")
        peaks_shared = sem("peaks_shared")
        scales_ready = sem("scales_ready")
        w_scaled = sem("w_scaled")
        w_hi_ready = sem("w_hi_ready")
        w_lo_ready = sem("w_lo_ready")
        ey_ready = sem("ey_ready")
        e_transposed = sem("e_transposed")
        eyT_ready = sem("eyT_ready")
        mod_sum = sem("mod_sum")
        mod_ready = sem("mod_ready")
        x2_nat = sem("x2_nat")
        staged2 = sem("staged2")
        x2_transposed = sem("x2_transposed")
        x2T_ready = sem("x2T_ready")
        x2_hi_ready = sem("x2_hi_ready")
        x2_split = sem("x2_split")
        r_sum = sem("r_sum")
        z_sum = sem("z_sum")
        c_sum = sem("c_sum")
        p_sum = sem("p_sum")
        r_ready = sem("r_ready")
        z_ready = sem("z_ready")
        c_ready = sem("c_ready")
        p_ready = sem("p_ready")
        rh_ready = sem("rh_ready")
        rh_hi_ready = sem("rh_hi_ready")
        rh_split = sem("rh_split")
        zh_ready = sem("zh_ready")
        keep_ready = sem("keep_ready")
        zc_ready = sem("zc_ready")
        h2_ready = sem("h2_ready")
        h2_hi_ready = sem("h2_hi_ready")
        h2_split_p = sem("h2_split_p")
        h2_next = sem("h2_next")
        x3_ready = sem("x3_ready")
        x3_hi_ready = sem("x3_hi_ready")
        x3_split = sem("x3_split")
        hid_sum = sem("hid_sum")
        out_sum = sem("out_sum")
        mem_sum = sem("mem_sum")
        hid_ready = sem("hid_ready")
        out_ready = sem("out_ready")
        mem_h_ready = sem("mem_h_ready")
        mem_ready = sem("mem_ready")
        m_ready = sem("m_ready")
        oh_ready = sem("oh_ready")
        om_ready = sem("om_ready")
        h3_ready = sem("h3_ready")
        h3_hi_ready = sem("h3_hi_ready")
        h3_split = sem("h3_split")
        x4_ready = sem("x4_ready")
        x4_transposed = sem("x4_transposed")
        x4_nat = sem("x4_nat")
        stored = sem("stored")

        def valid(t, off=0):
            return t is None or 0 <= t + off < T

        block = ctx.enter_context(nc.Block())

        @block.sync
        def _(sp):
            GC = UNROLL * D
            xv = a["x"].rearrange("b t d -> b (t d)")
            ov = out.rearrange("b t d -> b (t d)")
            sp.dma_start(X[:, 0:GC], xv[:, 0:GC]).then_inc(x_loaded, 16)
            sp.wait_ge(x_loaded, 16)
            sp.dma_start(X[:, GC:2 * GC], xv[:, GC:2 * GC]).then_inc(x_loaded, 16)
            for first, name, n in ((Z0, "L2_cond_Wz", 2), (R0, "L2_cond_Wr", 2), (C0, "L2_cond_Wh", 2),
                                   (G0, "L3_cond_w_W", 4), (P0, "L2_cond_Wp", 1), (MX0, "L3_cond_wx_W", 1),
                                   (MH0, "L3_cond_wh_W", 1)):
                src = a[name].rearrange("(c p) n -> p c n", p=P)
                sp.dma_start(W[:, first * CW:(first + n) * CW].rearrange("p (c n) -> p c n", n=src.shape[2]),
                             src).then_inc(weights_loaded, 16)
            for dst, name in ((bz, "L2_cond_bz"), (br, "L2_cond_br"), (bc, "L2_cond_bh"), (bp, "L2_cond_bp"),
                              (bg, "L3_cond_w_b"), (bx, "L3_cond_wx_b"), (bm, "L3_cond_wh_b")):
                sp.dma_start(dst[:, :], a[name].rearrange("(c p) -> p c", p=P),
                             allow_slow_non_contiguous=True).then_inc(weights_loaded, 16)
            with sp.Fori(2, GROUPS) as g:
                sp.wait_ge(x_loaded, g * 16)
                sp.dma_start(X[:, bass.ds(g * GC, GC)], xv[:, bass.ds(g * GC, GC)]).then_inc(x_loaded, 16)
            sp.wait_ge(x4_nat, UNROLL)
            sp.dma_start(ov[:, 0:GC], X[:, 0:GC]).then_inc(stored, 16)
            with sp.Fori(1, GROUPS) as g:
                sp.wait_ge(x4_nat, g * UNROLL + UNROLL)
                sp.dma_start(ov[:, bass.ds(g * GC, GC)], X[:, bass.ds(g * GC, GC)]).then_inc(stored, 16)
            sp.wait_ge(stored, 16 * GROUPS)

        @block.gpsimd
        def _(pool):
            pool.memset(ident[:, :], 0.0).then_inc(ident_zero, 1)
            pool.memset(W[:, (CHUNKS - 1) * CW:], 0.0).then_inc(pad_ready, 1)
            pool.memset(ones[:, :], 1.0).then_inc(ones_ready, 1)
            pool.wait_ge(ident_zero, 1)
            pool.affine_select(out=ident[:, :], in_=ident[:, :], compare_op=ALU.not_equal, fill=1.0,
                               base=0, pattern=[[-1, P]], channel_multiplier=1).then_inc(ident_ready, 1)

            def rnn(t, j, n, pos):
                if valid(t, 3):
                    s = (j + 3) % 2
                    if t is None or t + 3 >= 2:
                        pool.wait_ge(x_transposed, n(2))
                    if (j + 3) % UNROLL == 0:
                        if t is None:
                            pool.wait_ge(x_loaded, (pos + 3) * (16 // UNROLL) + 16)
                        else:
                            pool.wait_ge(x_loaded, 16 * ((t + 3) // UNROLL + 1))
                    pool.tensor_tensor(stage[:, s, :], X[:, bass.ds((pos + 3) * D, D)], ones[:, :],
                                       ALU.mult).then_inc(staged, 1)

            pool.wait_ge(ones_ready, 1)
            for t in range(-3, UNROLL):
                rnn(t, t % UNROLL, lambda k, t=t: t + k, t)
            with pool.Fori(1, GROUPS - 1) as i:
                base = Count(pool, i * UNROLL)
                for j in range(UNROLL):
                    rnn(None, j, lambda k, j=j: base(j + k), i * UNROLL + j)
            def share_peaks(nth, first, end):
                pool.wait_ge(peaks_ready, nth)
                pool.partition_all_reduce(peak_all[:, first:end], peak[:, first:end], P,
                                          bass.bass_isa.ReduceOp.max).then_inc(peaks_shared, 1)

            rnn(T - UNROLL, 0, lambda k: T - UNROLL + k, T - UNROLL)
            share_peaks(1, 0, CHUNKS)

            def modulate(t, j, n, pos):
                if valid(t, 2):
                    if t is None or t >= 0:
                        pool.wait_ge(e_transposed, n(1))
                    pool.tensor_tensor(ey[:, j % 2, :], X_il[:, :, bass.ds(pos + 2, 1)], cond[:, :],
                                       ALU.mult).then_inc(ey_ready, 1)

            pool.wait_ge(x1_ready, T)
            pool.wait_ge(cond_loaded, 16)
            for t in range(-2, UNROLL):
                modulate(t, t % UNROLL, lambda k, t=t: t + k, t)
            share_peaks(2, CHUNKS, CHUNKS + 2)
            with pool.Fori(1, GROUPS - 1) as i:
                base = Count(pool, i * UNROLL)
                for j in range(UNROLL):
                    modulate(None, j, lambda k, j=j: base(j + k), i * UNROLL + j)
            for t in range(T - UNROLL, T):
                modulate(t, t % UNROLL, lambda k, t=t: t + k, t)

            def bring(pos, ahead, slot, freed):
                if freed is not None:
                    pool.wait_ge(x2_transposed, freed)
                pool.tensor_tensor(stage[:, slot % 2, :], X[:, bass.ds((pos + ahead) * D, D)], ones[:, :],
                                   ALU.mult).then_inc(staged2, 1)

            def gates(t, j, n, pos):
                if valid(t):
                    h = h2p[:, :] if j == 0 and (t is None or t > 0) else h2[:, (j + 1) % 2, :]
                    pool.wait_ge(z_ready, n(1))
                    pool.tensor_tensor(zh[:, :], zT[:, :], h, ALU.mult).then_inc(zh_ready, 1)
                    pool.wait_ge(zh_ready, n(1))
                    pool.tensor_tensor(keep[:, :], h, zh[:, :], ALU.subtract).then_inc(keep_ready, 1)
                if valid(t, -2):
                    pool.wait_ge(h3_ready, n(-1))
                    if t is None or t >= 4:
                        pool.wait_ge(x4_transposed, n(-3))
                    pool.tensor_tensor(x4T[:, j % 2, :], x3T[:, (j + 2) % UNROLL, :], h3[:, j % 2, :],
                                       ALU.add).then_inc(x4_ready, 1)
                if valid(t):
                    pool.wait_ge(h2_ready, n(1))
                    pool.tensor_tensor(x3T[:, j, :], x2T[:, j % 2, :], h2[:, j % 2, :], ALU.add
                                       ).then_inc(x3_ready, 1)
                    pool.wait_ge(x3_hi_ready, n(1))
                    pool.tensor_tensor(x3_lo[:, :], x3T[:, j, :], x3_hi[:, :], ALU.subtract
                                       ).then_inc(x3_split, 1)
                if valid(t, -1):
                    pool.wait_ge(out_ready, n(0))
                    pool.tensor_tensor(oh[:, :], outT[:, :], h3[:, j % 2, :], ALU.mult)
                    pool.tensor_scalar(one_o[:, :], outT[:, :], -1.0, 1.0, ALU.mult, ALU.add
                                       ).then_inc(oh_ready, 1)
                if valid(t, 3):
                    bring(pos, 3, j + 1, None if t is not None and t < -1 else n(2))

            pool.wait_ge(x2_nat, L)
            for t in range(-3, UNROLL):
                gates(t, t % UNROLL, lambda k, t=t: t + k, t)
            with pool.Fori(1, GROUPS - 1) as i:
                base = Count(pool, i * UNROLL)
                for j in range(UNROLL):
                    gates(None, j, lambda k, j=j: base(j + k), i * UNROLL + j)
            for t in range(T - UNROLL, T + 3):
                gates(t, t % UNROLL, lambda k, t=t: t + k, t)

        @block.scalar
        def _(act):
            act.dma_start(wx0[:, :, :], a["L0_cond_Wx"].rearrange("(c p) n -> p c n", p=P)).then_inc(wx_loaded, 16)
            act.dma_start(cond[:, :], a["cond_1024"]).then_inc(cond_loaded, 16)
            act.dma_start(wh0[:, :, :], a["L0_cond_Wh"].rearrange("(c p) n -> p c n", p=P)).then_inc(wh_loaded, 16)
            act.dma_start(b0[:, :], a["L0_cond_b"].rearrange("(c p) -> p c", p=P),
                          allow_slow_non_contiguous=True).then_inc(b0_loaded, 16)
            act.dma_start(w1[:, :, :], a["L1_cond_weight"].rearrange("e (c p) i f -> p c (e i f)", p=P)
                          ).then_inc(w1_loaded, 16)
            act.wait_ge(ones_ready, 1)
            nc.scalar.activation(warm[:, :], ones[:, 0:1], ACT.Sigmoid)

            def rnn(t, j, n, pos):
                if valid(t):
                    act.wait_ge(rnn_sum, n(1))
                    for f in range(KC):
                        nc.scalar.activation(h0T[:, j % 2, f, :], pre[j % 2][:, f * B:(f + 1) * B], ACT.Tanh,
                                             bias=b0[:, f:f + 1]).then_inc(rnn_h[f], 1)

            act.wait_ge(b0_loaded, 16)
            for t in range(UNROLL):
                rnn(t, t % UNROLL, lambda k, t=t: t + k, t)
            with act.Fori(1, GROUPS - 1) as i:
                base = Count(act, i * UNROLL)
                for j in range(UNROLL):
                    rnn(None, j, lambda k, j=j: base(j + k), i * UNROLL + j)
            for t in range(T - UNROLL, T):
                rnn(t, t % UNROLL, lambda k, t=t: t + k, t)

            def modulate(t, j, n, pos):
                if valid(t, 2):
                    act.wait_ge(e_transposed, n(3))
                    nc.scalar.activation(eyT[:, j % 2, :, :].rearrange("p c b -> p (c b)"),
                                         tin[j % 2][:, 0:KC * B], ACT.Copy).then_inc(eyT_ready, 1)

            for t in range(-2, UNROLL):
                modulate(t, t % UNROLL, lambda k, t=t: t + k, t)
            act.wait_ge(scales_ready, 1)
            act.wait_ge(weights_loaded, 16 * 14)
            with act.Fori(1, GROUPS - 1) as i:
                base = Count(act, i * UNROLL)
                done = act.snap(i)
                for j in range(UNROLL):
                    modulate(None, j, lambda k, j=j: base(j + k), i * UNROLL + j)
                    chunk = W[:, bass.ds(i * CW - CW, CW)]
                    if j == 0:
                        nc.scalar.activation(chunk, chunk, ACT.Copy,
                                             scale=chunk_scale[:, bass.ds(i - 1, 1)]).then_inc(w_scaled, 1)
                    if j == 2:
                        act.wait_ge(w_scaled, done)
                        nc.scalar.activation(W_hi[:, bass.ds(i * CW - CW, CW)], chunk, ACT.Copy
                                             ).then_inc(w_hi_ready, 1)
            for t in range(T - UNROLL, T):
                modulate(t, t % UNROLL, lambda k, t=t: t + k, t)

            act.wait_ge(scales_ready, 2)

            def gate(dst, src, func, column, b, ready):
                for f in range(KC):
                    last = nc.scalar.activation(dst[:, f * B:(f + 1) * B], src[:, f * B:(f + 1) * B], func,
                                                bias=b[:, f:f + 1], scale=undo_sum[:, column:column + 1])
                last.then_inc(ready, 1)

            def gates(t, j, n, pos):
                if valid(t):
                    act.wait_ge(r_sum, n(1))
                    gate(rT, R_ps, ACT.Sigmoid, SR, br, r_ready)
                if valid(t):
                    act.wait_ge(z_sum, n(1))
                    gate(zT, Z_ps, ACT.Sigmoid, SZ, bz, z_ready)
                if valid(t, 1):
                    act.wait_ge(x2_transposed, n(2))
                    if t is None or t >= 1:
                        act.wait_ge(x3_ready, n(0))
                    nc.scalar.activation(x2T[:, (j + 1) % 2, :], XIN_ps[:, 0:KC * B], ACT.Copy,
                                         scale=scale[:, SA:SA + 1]).then_inc(x2T_ready, 1)
                if valid(t, -3):
                    act.wait_ge(x4_transposed, n(-2))
                    nc.scalar.activation(X[:, bass.ds((pos - 3) * D, D)], XOUT_ps[:, 0:D], ACT.Copy,
                                         scale=undo[:, SA:SA + 1]).then_inc(x4_nat, 1)
                if valid(t):
                    act.wait_ge(c_sum, n(1))
                    gate(cT, C_ps, ACT.Tanh, SC, bc, c_ready)
                if valid(t, -1):
                    act.wait_ge(hid_sum, n(0))
                    gate(hidT, HID_ps, ACT.Sigmoid, SG, bg, hid_ready)
                    act.wait_ge(out_sum, n(0))
                    gate(outT, OUT_ps, ACT.Sigmoid, SG, bg[:, KC:], out_ready)
                if valid(t) and j == UNROLL - 1 and (t is None or t < T - 1):
                    act.wait_ge(p_sum, (pos + 1) // UNROLL if t is not None else group(pos))
                    gate(pT, P_ps, ACT.Tanh, SP, bp, p_ready)
                if valid(t, -1):
                    act.wait_ge(mem_ready, n(0))
                    gate(mT, mem, ACT.Tanh, SM, bx, m_ready)

            for t in range(-2, UNROLL):
                group = None
                gates(t, t % UNROLL, lambda k, t=t: t + k, t)
            with act.Fori(1, GROUPS - 1) as i:
                base = Count(act, i * UNROLL)
                nth = act.snap(i + 1)
                group = lambda pos: nth
                for j in range(UNROLL):
                    gates(None, j, lambda k, j=j: base(j + k), i * UNROLL + j)
            for t in range(T - UNROLL, T + 3):
                gates(t, t % UNROLL, lambda k, t=t: t + k, t)

        @block.vector
        def _(dve):
            def rnn(t, j, n, pos):
                if valid(t, 2):
                    dve.wait_ge(x_transposed, n(3))
                    nc.vector.tensor_copy(xT[:, j % 2, :, :].rearrange("p c b -> p (c b)"),
                                          tin[j % 2][:, 0:KC * B]).then_inc(xT_ready, 1)
                if t == -2:
                    dve.wait_ge(cond_transposed, 1)
                    nc.vector.tensor_copy(condT[:, :, :].rearrange("p c b -> p (c b)"), setup_ps[0][:, 0:KC * B]
                                          ).then_inc(condT_ready, 1)
                if valid(t, -1):
                    dve.wait_ge(h_transposed, n(0))
                    x1 = X[:, bass.ds((pos - 1) * D, D)]
                    nc.vector.tensor_tensor(x1, tout[(j + 1) % 2][:, 0:D], x1, ALU.add).then_inc(x1_ready, 1)
                if valid(t, -2):
                    dve.wait_ge(x1_ready, n(-1))
                    nc.vector.tensor_reduce(xmax[:, bass.ds(pos - 2, 1)], X[:, bass.ds((pos - 2) * D, D)],
                                            AX, ALU.max, apply_absolute_value=True).then_inc(xmax_ready, 1)

            chain = [0]

            def link(ins):
                chain[0] += 1
                ins.then_inc(setup_step, 1)
                dve.wait_ge(setup_step, chain[0])

            def flat(tile):
                return tile[:, :, :].rearrange("p c n -> p (c n)")

            def squares():
                dve.wait_ge(w1_transposed, 1)
                nc.vector.tensor_copy(flat(w1T), setup_ps[1][:, 0:CW]).then_inc(w1T_ready, 1)
                nc.vector.tensor_tensor(flat(condT2), flat(condT), flat(condT), ALU.mult)
                dve.wait_ge(w1T_ready, 1)
                nc.vector.tensor_tensor(flat(w1T2), flat(w1T), flat(w1T), ALU.mult).then_inc(w1T_ready, 1)

            def first_guess():
                dve.wait_ge(norm_sum, 1)
                link(nc.vector.tensor_scalar(norm_v[:, :], setup_ps[0][:, 0:D], 1.0 / D, 1e-8, ALU.mult, ALU.add))
                link(nc.vector.tensor_scalar(norm_r[:, :].bitcast(I32), norm_v[:, :].bitcast(I32), -0.5,
                                             float(0x5F3759DF), ALU.mult, ALU.add))

            def refine():
                link(nc.vector.tensor_tensor(norm_q[:, :], norm_r[:, :], norm_r[:, :], ALU.mult))
                link(nc.vector.scalar_tensor_tensor(norm_q[:, :], norm_q[:, :], -0.5, norm_v[:, :],
                                                    ALU.mult, ALU.mult))
                link(nc.vector.scalar_tensor_tensor(norm_r[:, :], norm_q[:, :], 1.5, norm_r[:, :],
                                                    ALU.add, ALU.mult))

            def widest(column, first, count):
                return nc.vector.tensor_reduce(top[:, column:column + 1], peak_all[:, first:first + count], AX,
                                               ALU.max)

            def power_of_two(first, end, least, e):
                at = slice(first, end)
                link(nc.vector.tensor_scalar(top[:, at], top[:, at], least, None, ALU.max))
                link(nc.vector.tensor_scalar(power[:, at].bitcast(I32), top[:, at].bitcast(I32), 0x7F800000, None,
                                             ALU.bitwise_and))
                nc.vector.tensor_scalar(scale[:, at].bitcast(I32), power[:, at].bitcast(I32), -1.0,
                                        float((254 + e) << 23), ALU.mult, ALU.add)
                link(nc.vector.tensor_scalar(undo[:, at], power[:, at], 2.0 ** -e, None, ALU.mult))

            def weight_scales():
                dve.wait_ge(peaks_shared, 1)
                for column, first, count in ((SZ, Z0, 2), (SR, R0, 2), (SC, C0, 2), (SG, G0, 4), (SP, P0, 1)):
                    widest(column, first, count)
                link(widest(SM, MX0, 2))
                power_of_two(0, SA, 2.0 ** -100, W_EXP)
                for c0, count, column in ((Z0, 2, SZ), (R0, 2, SR), (C0, 2, SC), (G0, 4, SG), (P0, 1, SP),
                                          (MX0, 3, SM)):
                    last = nc.vector.tensor_copy(chunk_scale[:, c0:c0 + count],
                                                 scale[:, column:column + 1].to_broadcast([P, count]))
                last.then_inc(scales_ready, 1)

            def activation_scale():
                dve.wait_ge(peaks_shared, 2)
                link(widest(SA, XMAX, 2))
                power_of_two(SA, NS, 1.0, A_EXP)
                nc.vector.tensor_scalar(undo_sum[:, :], undo[:, :], undo[:, SA:SA + 1], None, ALU.mult)
                link(nc.vector.tensor_scalar(scale_m[:, :], scale[:, SM:SM + 1], scale[:, SA:SA + 1], None,
                                             ALU.mult))
                nc.vector.tensor_scalar(bm_s[:, :], bm[:, :], scale_m[:, :], None, ALU.mult).then_inc(scales_ready, 1)

            for t in range(-2, UNROLL):
                rnn(t, t % UNROLL, lambda k, t=t: t + k, t)
                if t == 1:
                    squares()
            first_guess()

            dve.wait_ge(weights_loaded, 16 * 14)
            dve.wait_ge(pad_ready, 1)
            with dve.Fori(1, GROUPS - 1) as i:
                base = Count(dve, i * UNROLL)
                for j in range(UNROLL):
                    rnn(None, j, lambda k, j=j: base(j + k), i * UNROLL + j)
                nc.vector.tensor_reduce(peak[:, bass.ds(i - 1, 1)], W[:, bass.ds(i * CW - CW, CW)], AX, ALU.max,
                                        apply_absolute_value=True)
            nc.vector.tensor_reduce(peak[:, HMAX:HMAX + 1], cond[:, :], AX, ALU.max, apply_absolute_value=True
                                    ).then_inc(peaks_ready, 1)
            for t in range(T - UNROLL, T + 2):
                rnn(t, t % UNROLL, lambda k, t=t: t + k, t)
                if t == T - 3:
                    weight_scales()
                elif t in (T - 4, T - 2, T):
                    refine()
            dve.wait_ge(xmax_ready, T)
            nc.vector.tensor_reduce(peak[:, XMAX:XMAX + 1], xmax[:, :], AX, ALU.max).then_inc(peaks_ready, 1)
            link(nc.vector.tensor_scalar(gain[:, :], norm_r[:, :], float(D) ** -0.5, None, ALU.mult))

            def modulate(t, j, n, pos):
                if valid(t):
                    dve.wait_ge(mod_sum, n(1))
                    if t is None or t >= 2:
                        dve.wait_ge(x2_nat, n(-1))
                    nc.vector.tensor_tensor(mod[:, j % 2, :], mod_ps[j % 2][:, 0:D], gain[:, :], ALU.mult
                                            ).then_inc(mod_ready, 1)
                if valid(t, -1):
                    dve.wait_ge(mod_ready, n(0))
                    x2 = X_il[:, :, bass.ds(pos - 1, 1)]
                    nc.vector.tensor_tensor(x2, mod[:, (j + 1) % 2, :], x2, ALU.add).then_inc(x2_nat, 1)

            for t in range(UNROLL):
                modulate(t, t % UNROLL, lambda k, t=t: t + k, t)
            activation_scale()
            with dve.Fori(1, GROUPS - 1) as i:
                base = Count(dve, i * UNROLL)
                chunks = dve.snap(i)
                for j in range(UNROLL):
                    modulate(None, j, lambda k, j=j: base(j + k), i * UNROLL + j)
                dve.wait_ge(w_hi_ready, chunks)
                nc.vector.tensor_tensor(W_lo[:, bass.ds(i * CW - CW, CW)], W[:, bass.ds(i * CW - CW, CW)],
                                        W_hi[:, bass.ds(i * CW - CW, CW)], ALU.subtract).then_inc(w_lo_ready, 1)
            for t in range(T - UNROLL, T + 1):
                modulate(t, t % UNROLL, lambda k, t=t: t + k, t)

            for dst in (h2, h3):
                last = nc.vector.tensor_scalar(dst[:, 1, :], condT[:, :, :].rearrange("p c b -> p (c b)"),
                                               scale[:, SA:SA + 1], None, ALU.mult)
            link(last)
            nc.vector.tensor_copy(h2_hi[:, :], h2[:, 1, :])
            nc.vector.tensor_copy(h3_hi[:, :], h3[:, 1, :]).then_inc(h3_hi_ready, 1)
            dve.wait_ge(h3_hi_ready, 1)
            nc.vector.tensor_tensor(h2_lo[:, :], h2[:, 1, :], h2_hi[:, :], ALU.subtract).then_inc(h2_next, 1)
            nc.vector.tensor_tensor(h3_lo[:, :], h3[:, 1, :], h3_hi[:, :], ALU.subtract).then_inc(h3_split, 1)

            def gates(t, j, n, pos):
                if valid(t):
                    h = h2p[:, :] if j == 0 and (t is None or t > 0) else h2[:, (j + 1) % 2, :]
                    dve.wait_ge(r_ready, n(1))
                    nc.vector.tensor_tensor(rh[:, :], rT[:, :], h, ALU.mult).then_inc(rh_ready, 1)
                if valid(t, -2):
                    dve.wait_ge(m_ready, n(-1))
                    dve.wait_ge(oh_ready, n(-1))
                    nc.vector.scalar_tensor_tensor(om[:, :], mT[:, :], scale[:, SA:SA + 1], one_o[:, :],
                                                   ALU.mult, ALU.mult).then_inc(om_ready, 1)
                if valid(t):
                    dve.wait_ge(rh_ready, n(1))
                    nc.vector.tensor_copy(rh_hi[:, :], rh[:, :]).then_inc(rh_hi_ready, 1)
                if valid(t, -2):
                    dve.wait_ge(om_ready, n(-1))
                    nc.vector.tensor_tensor(h3[:, j % 2, :], om[:, :], oh[:, :], ALU.add).then_inc(h3_ready, 1)
                if valid(t):
                    dve.wait_ge(rh_hi_ready, n(1))
                    nc.vector.tensor_tensor(rh_lo[:, :], rh[:, :], rh_hi[:, :], ALU.subtract
                                            ).then_inc(rh_split, 1)
                if valid(t, -2):
                    dve.wait_ge(h3_ready, n(-1))
                    nc.vector.tensor_copy(h3_hi[:, :], h3[:, j % 2, :]).then_inc(h3_hi_ready, 1)
                if valid(t, 1):
                    dve.wait_ge(x2T_ready, n(2))
                    if t is None or t >= 0:
                        dve.wait_ge(r_sum, n(1))
                    nc.vector.tensor_copy(x2_hi[:, :], x2T[:, (j + 1) % 2, :]).then_inc(x2_hi_ready, 1)
                if valid(t, -2):
                    dve.wait_ge(h3_hi_ready, n(0))
                    nc.vector.tensor_tensor(h3_lo[:, :], h3[:, j % 2, :], h3_hi[:, :], ALU.subtract
                                            ).then_inc(h3_split, 1)
                if valid(t, 1):
                    dve.wait_ge(x2_hi_ready, n(2))
                    nc.vector.tensor_tensor(x2_lo[:, :], x2T[:, (j + 1) % 2, :], x2_hi[:, :], ALU.subtract
                                            ).then_inc(x2_split, 1)
                if valid(t):
                    dve.wait_ge(c_ready, n(1))
                    nc.vector.scalar_tensor_tensor(zc[:, :], cT[:, :], scale[:, SA:SA + 1], zT[:, :],
                                                   ALU.mult, ALU.mult).then_inc(zc_ready, 1)
                    dve.wait_ge(keep_ready, n(1))
                    dve.wait_ge(zc_ready, n(1))
                    nc.vector.tensor_tensor(h2[:, j % 2, :], zc[:, :], keep[:, :], ALU.add).then_inc(h2_ready, 1)
                    if t is None or t < T - 1:
                        dve.wait_ge(h2_ready, n(1))
                        nc.vector.tensor_copy(h2_hi[:, :], h2[:, j % 2, :]).then_inc(h2_hi_ready, 1)
                        dve.wait_ge(h2_hi_ready, pairs(t, j, pos))
                        nc.vector.tensor_tensor(h2_lo[:, :], h2[:, j % 2, :], h2_hi[:, :], ALU.subtract
                                                ).then_inc(h2_split_p if j == UNROLL - 1 else h2_next, 1)
                if valid(t):
                    dve.wait_ge(x3_ready, n(1))
                    nc.vector.tensor_copy(x3_hi[:, :], x3T[:, j, :]).then_inc(x3_hi_ready, 1)
                if valid(t, -1):
                    dve.wait_ge(mem_sum, n(0))
                    dve.wait_ge(hid_ready, n(0))
                    for f in range(KC):
                        at = slice(f * B, (f + 1) * B)
                        last = nc.vector.scalar_tensor_tensor(mem_h[:, at], M_ps[:, KC * B + f * B:KC * B + (f + 1) * B],
                                                              bm_s[:, f:f + 1], hidT[:, at], ALU.add, ALU.mult)
                    last.then_inc(mem_h_ready, 1)
                    dve.wait_ge(mem_h_ready, n(0))
                    nc.vector.tensor_tensor(mem[:, :], M_ps[:, 0:KC * B], mem_h[:, :], ALU.add
                                            ).then_inc(mem_ready, 1)
                if valid(t) and j == UNROLL - 1 and (t is None or t < T - 1):
                    dve.wait_ge(p_ready, nth(t, pos))
                    nc.vector.tensor_scalar(h2_hi[:, :], pT[:, :], scale[:, SA:SA + 1], None, ALU.mult
                                            ).then_inc(h2_hi_ready, 1)
                    nc.vector.tensor_scalar(h2p[:, :], pT[:, :], scale[:, SA:SA + 1], None, ALU.mult)
                    dve.wait_ge(h2_hi_ready, pairs(t, j, pos, 1))
                    nc.vector.scalar_tensor_tensor(h2_lo[:, :], pT[:, :], scale[:, SA:SA + 1], h2_hi[:, :],
                                                   ALU.mult, ALU.subtract).then_inc(h2_next, 1)

            known = {}

            def nth(t, pos):
                return (t + 1) // UNROLL if t is not None else known["nth"]

            def pairs(t, j, pos, more=0):
                if t is not None:
                    return t // UNROLL * (UNROLL + 1) + j + 1 + more
                if j + more not in known:
                    known[j + more] = dve.snap(known["i"] * (UNROLL + 1) + (j + more + 1))
                return known[j + more]

            for t in range(-2, UNROLL):
                gates(t, t % UNROLL, lambda k, t=t: t + k, t)
            with dve.Fori(1, GROUPS - 1) as i:
                base = Count(dve, i * UNROLL)
                known.clear()
                known["i"] = i
                known["nth"] = dve.snap(i + 1)
                for j in range(UNROLL):
                    gates(None, j, lambda k, j=j: base(j + k), i * UNROLL + j)
            for t in range(T - UNROLL, T + 3):
                gates(t, t % UNROLL, lambda k, t=t: t + k, t)

        @block.tensor
        def _(pe):
            def mm(dst, lhsT, rhs, start=False):
                return nc.tensor.matmul(dst, lhsT, rhs, start=start, stop=True, skip_group_check=True)

            def transposed(dst, src):
                for c in range(KC):
                    last = nc.tensor.transpose(dst[:, c * P:(c + 1) * P], src[:, c * P:(c + 1) * P], ident[:, :])
                return last

            def keep_warm(count, bank):
                for _ in range(count):
                    nc.tensor.transpose(bank[:, 0:P], ident[:, :], ident[:, :])

            def rnn(t, j, n, pos):
                if valid(t):
                    for k in range(KC):
                        if t == 0:
                            pe.wait_ge(condT_ready, 1)
                            pe.wait_ge(wh_loaded, 16)
                            h = condT[:, k, :]
                        else:
                            pe.wait_ge(rnn_h[k], n(0))
                            h = h0T[:, (j + 1) % 2, k, :]
                        for f in range(KC):
                            last = mm(pre[j % 2][:, f * B:(f + 1) * B], wh0[:, k, f * P:(f + 1) * P], h)
                    last.then_inc(rnn_sum, 1)
                if valid(t, 1):
                    if t == -1:
                        pe.wait_ge(wx_loaded, 16)
                    pe.wait_ge(xT_ready, n(2))
                    for k in range(KC):
                        for f in range(KC):
                            mm(pre[(j + 1) % 2][:, f * B:(f + 1) * B], wx0[:, k, f * P:(f + 1) * P],
                               xT[:, (j + 1) % 2, k, :], start=(k == 0 and f == 0))
                if valid(t, 2):
                    pe.wait_ge(staged, n(3))
                    if t is None or t >= 0:
                        pe.wait_ge(xT_ready, n(1))
                    transposed(tin[j % 2], stage[:, j % 2, :]).then_inc(x_transposed, 1)
                if t == -2:
                    pe.wait_ge(cond_loaded, 16)
                    transposed(setup_ps[0], cond).then_inc(cond_transposed, 1)
                if valid(t, -1):
                    if t == T:
                        for k in range(KC):
                            pe.wait_ge(rnn_h[k], T)
                    if t is None or t >= 3:
                        pe.wait_ge(x1_ready, n(-2))
                    transposed(tout[(j + 1) % 2], h0T[:, (j + 1) % 2, :, :].rearrange("p c b -> p (c b)")
                               ).then_inc(h_transposed, 1)

            pe.wait_ge(ident_ready, 1)
            keep_warm(12, setup_ps[0])
            for t in range(-2, UNROLL):
                rnn(t, t % UNROLL, lambda k, t=t: t + k, t)
                if t == 1:
                    pe.wait_ge(w1_loaded, 16)
                    for c in range(KC):
                        for o in range(KC):
                            last = nc.tensor.transpose(setup_ps[1][:, c * D + o * P:c * D + (o + 1) * P],
                                                       w1[:, o, c * P:(c + 1) * P], ident[:, :])
                    last.then_inc(w1_transposed, 1)
            pe.wait_ge(w1T_ready, 2)
            for k in range(KC):
                last = mm(setup_ps[0][:, 0:D], condT2[:, k, :], w1T2[:, k, :], start=(k == 0))
            last.then_inc(norm_sum, 1)

            with pe.Fori(1, GROUPS - 1) as i:
                base = Count(pe, i * UNROLL)
                for j in range(UNROLL):
                    rnn(None, j, lambda k, j=j: base(j + k), i * UNROLL + j)
            for t in range(T - UNROLL, T + 1):
                rnn(t, t % UNROLL, lambda k, t=t: t + k, t)

            keep_warm(24, setup_ps[0])

            def modulate(t, j, n, pos):
                if valid(t):
                    pe.wait_ge(eyT_ready, n(1))
                    if t is None or t >= 2:
                        pe.wait_ge(mod_ready, n(-1))
                    for k in range(KC):
                        last = mm(mod_ps[j % 2][:, 0:D], eyT[:, j % 2, k, :], w1T[:, k, :], start=(k == 0))
                    last.then_inc(mod_sum, 1)
                if valid(t, 2):
                    pe.wait_ge(ey_ready, n(3))
                    if t is None or t >= 0:
                        pe.wait_ge(eyT_ready, n(1))
                    transposed(tin[j % 2], ey[:, j % 2, :]).then_inc(e_transposed, 1)

            for t in range(-2, UNROLL):
                modulate(t, t % UNROLL, lambda k, t=t: t + k, t)
            with pe.Fori(1, GROUPS - 1) as i:
                base = Count(pe, i * UNROLL)
                for j in range(UNROLL):
                    modulate(None, j, lambda k, j=j: base(j + k), i * UNROLL + j)
            for t in range(T - UNROLL, T):
                modulate(t, t % UNROLL, lambda k, t=t: t + k, t)

            def product(dst, w_at, x_hi, x_lo, begins=False):
                for k in range(KC):
                    for f in range(KC):
                        c, at = w_at(k, f), slice(k * B, (k + 1) * B)
                        for w, x in ((W_hi, x_hi), (W_hi, x_lo), (W_lo, x_hi)):
                            last = mm(dst[:, f * B:(f + 1) * B], w[:, c:c + P], x[:, at], begins)
                            begins = False
                return last

            def high_part(dst, w_at, x_hi):
                for k in range(KC):
                    for f in range(KC):
                        for w in (W_hi, W_lo):
                            mm(dst[:, f * B:(f + 1) * B], w[:, w_at(k, f):w_at(k, f) + P], x_hi[:, k * B:(k + 1) * B])

            def low_part(dst, w_at, x_lo):
                for k in range(KC):
                    for f in range(KC):
                        last = mm(dst[:, f * B:(f + 1) * B], W_hi[:, w_at(k, f):w_at(k, f) + P],
                                  x_lo[:, k * B:(k + 1) * B])
                return last

            def block_at(chunk):
                return lambda k, f: chunk * CW + k * D + f * P

            def fused_at(half, part):
                return lambda k, f: (G0 + 2 * half + k) * CW + part * D + f * P

            def memory_of_x(t, n):
                pe.wait_ge(x3_split, n(0))
                if t is None or t >= 2:
                    pe.wait_ge(mem_ready, n(-1))
                product(M_ps, block_at(MX0), x3_hi, x3_lo, True)

            def gates(t, j, n, pos):
                if valid(t, -1) and j == 0:
                    memory_of_x(t, n)
                if valid(t):
                    pe.wait_ge(h2_next, n(1))
                    product(R_ps, block_at(R0 + 1), h2_hi, h2_lo).then_inc(r_sum, 1)
                    product(Z_ps, block_at(Z0 + 1), h2_hi, h2_lo).then_inc(z_sum, 1)
                if valid(t, -1):
                    if j > 0:
                        memory_of_x(t, n)
                    if t is None or t >= 2:
                        pe.wait_ge(hid_ready, n(-1))
                    product(HID_ps, fused_at(0, 0), x3_hi, x3_lo, True)
                    if t is None or t >= 2:
                        pe.wait_ge(out_ready, n(-1))
                    product(OUT_ps, fused_at(0, 1), x3_hi, x3_lo, True)
                if valid(t, 2):
                    pe.wait_ge(staged2, n(3))
                    if t is None or t >= -1:
                        pe.wait_ge(x2T_ready, n(2))
                    if j == 0 and (t is None or t > 0):
                        pe.wait_ge(p_ready, nth(t, j))
                    transposed(XIN_ps, stage[:, j % 2, :]).then_inc(x2_transposed, 1)
                if valid(t):
                    pe.wait_ge(rh_hi_ready, n(1))
                    high_part(C_ps, block_at(C0 + 1), rh_hi)
                    pe.wait_ge(rh_split, n(1))
                    low_part(C_ps, block_at(C0 + 1), rh_lo).then_inc(c_sum, 1)
                if valid(t, -1):
                    pe.wait_ge(h3_hi_ready, n(0))
                    high_part(HID_ps, fused_at(1, 0), h3_hi)
                    pe.wait_ge(h3_split, n(0))
                    low_part(HID_ps, fused_at(1, 0), h3_lo).then_inc(hid_sum, 1)
                    product(M_ps[:, KC * B:], block_at(MH0), h3_hi, h3_lo).then_inc(mem_sum, 1)
                    product(OUT_ps, fused_at(1, 1), h3_hi, h3_lo).then_inc(out_sum, 1)
                if valid(t, -2):
                    pe.wait_ge(x4_ready, n(-1))
                    if t is None or t >= 3:
                        pe.wait_ge(x4_nat, n(-2))
                    transposed(XOUT_ps, x4T[:, j % 2, :]).then_inc(x4_transposed, 1)
                if valid(t, 1):
                    pe.wait_ge(x2_split, n(2))
                    if t is None or t >= 0:
                        pe.wait_ge(z_ready, n(1))
                    product(Z_ps, block_at(Z0), x2_hi, x2_lo, True)
                if valid(t) and j == UNROLL - 1 and (t is None or t < T - 1):
                    pe.wait_ge(h2_split_p, nth(t, j))
                    product(P_ps, block_at(P0), h2_hi, h2_lo, True).then_inc(p_sum, 1)
                if valid(t, 1):
                    if t is None or t >= 0:
                        pe.wait_ge(c_ready, n(1))
                    product(C_ps, block_at(C0), x2_hi, x2_lo, True)
                    if t is None or t >= 0:
                        pe.wait_ge(r_ready, n(1))
                    product(R_ps, block_at(R0), x2_hi, x2_lo, True)

            known = {}

            def nth(t, j):
                return (t + 1) // UNROLL if t is not None else known["nth" if j else "before"]

            keep_warm(20, XOUT_ps)
            pe.wait_ge(w_lo_ready, CHUNKS)
            pe.wait_ge(mod_ready, L)
            for t in range(-2, UNROLL):
                gates(t, t % UNROLL, lambda k, t=t: t + k, t)
                if t == -2:
                    keep_warm(8, XOUT_ps)
            with pe.Fori(1, GROUPS - 1) as i:
                base = Count(pe, i * UNROLL)
                known["nth"], known["before"] = pe.snap(i + 1), pe.snap(i)
                for j in range(UNROLL):
                    gates(None, j, lambda k, j=j: base(j + k), i * UNROLL + j)
            for t in range(T - UNROLL, T + 3):
                gates(t, t % UNROLL, lambda k, t=t: t + k, t)


_INS = ["x", "cond_1024", "L0_cond_Wx", "L0_cond_Wh", "L0_cond_b", "L1_cond_weight", "L2_cond_Wz", "L2_cond_bz",
        "L2_cond_Wr", "L2_cond_br", "L2_cond_Wh", "L2_cond_bh", "L2_cond_Wp", "L2_cond_bp", "L3_cond_w_W",
        "L3_cond_w_b", "L3_cond_wx_W", "L3_cond_wx_b", "L3_cond_wh_W", "L3_cond_wh_b"]


def kernel(**inputs):
    import numpy as np
    import concourse.bacc as bacc
    from concourse.bass_utils import run_bass_kernel_spmd

    nc = bacc.Bacc("TRN2", target_bir_lowering=False, num_devices=1)
    arrays, aps = {}, {}
    for name in _INS:
        arr = np.ascontiguousarray(inputs[name])
        arrays[f"in_{name}"] = arr
        aps[name] = nc.dram_tensor(f"in_{name}", arr.shape, mybir.dt.from_np(arr.dtype), kind="ExternalInput").ap()
    out = nc.dram_tensor("out_x", arrays["in_x"].shape, F32, kind="ExternalOutput").ap()
    build_kernel(nc, aps, out)
    r = run_bass_kernel_spmd(nc, [arrays], core_ids=[0])
    return r.results[0]["out_x"]
```

```python
import concourse.bass as bass
from concourse import mybir
from concourse.alu_op_type import AluOpType as ALU
from contextlib import ExitStack

F32 = mybir.dt.float32
F16 = mybir.dt.float16
I32 = mybir.dt.int32
ACT = mybir.ActivationFunctionType
AX = mybir.AxisListType.X

P = 128
D = 256
KC = D // P
UNROLL = 4


class Count:

    def __init__(self, eng, first):
        self.eng, self.first, self.known = eng, first, {}

    def __call__(self, k):
        if isinstance(self.first, int):
            return self.first + k
        if k not in self.known:
            self.known[k] = self.eng.snap(self.first + k)
        return self.known[k]


def build_kernel(nc, a, out):
    B, T, _ = a["x"].shape
    L = T * D // D
    assert B == P and T % UNROLL == 0 and a["x"].shape[2] == D
    GROUPS = T // UNROLL

    W_EXP, A_EXP = 14, 9
    REFINEMENTS = 3
    H_SCALE = 2.0 ** 15

    CW = KC * D
    Z0, R0, C0, G0, P0, MX0, MH0, CHUNKS = 0, 2, 4, 6, 10, 11, 12, 14
    XMAX, HMAX = CHUNKS, CHUNKS + 1
    S0, SZ, SR, SC, SG, SP, SM, SA = range(8)
    NS = 8

    ctx = ExitStack()
    with ctx:
        def sb(name, shape, dt=F32):
            return ctx.enter_context(nc.sbuf_tensor(name, shape, dt))

        def sem(name):
            return ctx.enter_context(nc.semaphore(name))

        X = sb("X", [P, T * D])
        X_il = X[:, :].rearrange("p (i l) -> p i l", l=L)
        stage = sb("stage", [P, 2, D])
        xT = sb("xT", [P, 2, KC, 2, B])
        ident = sb("ident", [P, P])
        ones = sb("ones", [P, D])
        warm = sb("warm", [P, 1])
        cond = sb("cond", [P, D])
        condT = sb("condT", [P, KC, B])
        condT2 = sb("condT2", [P, KC, B])
        wx0 = sb("wx0", [P, KC, D])
        wh0 = sb("wh0", [P, KC, D])
        b0 = sb("b0", [P, KC])
        wx0_s = sb("wx0_s", [P, KC, D])
        wh0_hi = sb("wh0_hi", [P, KC, D], F16)
        wh0_lo = sb("wh0_lo", [P, KC, D], F16)
        peak0 = sb("peak0", [P, 2])
        peak0_all = sb("peak0_all", [P, 2])
        scale0 = sb("scale0", [P, 1])
        undo0 = sb("undo0", [P, 1])
        h0T = sb("h0T", [P, 2, KC, B])
        h0_hi = sb("h0_hi", [P, KC, B], F16)
        h0_lo = sb("h0_lo", [P, KC, B], F16)
        w1 = sb("w1", [P, KC, D])
        w1T = sb("w1T", [P, KC, D])
        w1T2 = sb("w1T2", [P, KC, D])
        norm_v = sb("norm_v", [P, D])
        norm_r = sb("norm_r", [P, D])
        norm_q = sb("norm_q", [P, D])
        gain = sb("gain", [P, D])
        ey = sb("ey", [P, 2, D])
        eyT = sb("eyT", [P, 2, KC, B])
        mod = sb("mod", [P, 2, D])
        W = sb("W", [P, CHUNKS * CW])
        W_hi = sb("W_hi", [P, CHUNKS * CW], F16)
        W_lo = sb("W_lo", [P, CHUNKS * CW], F16)
        bz = sb("bz", [P, KC])
        br = sb("br", [P, KC])
        bc = sb("bc", [P, KC])
        bp = sb("bp", [P, KC])
        bg = sb("bg", [P, 2 * KC])
        bx = sb("bx", [P, KC])
        bm = sb("bm", [P, KC])
        bm_s = sb("bm_s", [P, KC])
        xmax = sb("xmax", [P, T])
        peak = sb("peak", [P, CHUNKS + 2])
        peak_all = sb("peak_all", [P, CHUNKS + 2])
        top = sb("top", [P, NS])
        power = sb("power", [P, NS])
        scale = sb("scale", [P, NS])
        undo = sb("undo", [P, NS])
        undo_sum = sb("undo_sum", [P, NS])
        scale_m = sb("scale_m", [P, 1])
        chunk_scale = sb("chunk_scale", [P, CHUNKS])
        x2T = sb("x2T", [P, UNROLL, KC * B])
        x2_hi = sb("x2_hi", [P, KC, 2, B], F16)
        x2_lo = sb("x2_lo", [P, KC, 2, B], F16)
        rT = sb("rT", [P, KC * B])
        zT = sb("zT", [P, KC * B])
        cT = sb("cT", [P, KC * B])
        rh = sb("rh", [P, KC * B])
        rh_hi = sb("rh_hi", [P, KC * B], F16)
        rh_lo = sb("rh_lo", [P, KC * B], F16)
        zh = sb("zh", [P, KC * B])
        keep = sb("keep", [P, KC * B])
        zc = sb("zc", [P, KC * B])
        h2 = sb("h2", [P, 2, KC * B])
        h2p = sb("h2p", [P, KC * B])
        pT = sb("pT", [P, KC * B])
        h2_hi = sb("h2_hi", [P, KC * B], F16)
        h2_lo = sb("h2_lo", [P, KC * B], F16)
        x3T = sb("x3T", [P, UNROLL, KC * B])
        x3_hi = sb("x3_hi", [P, 2, KC, 2, B], F16)
        x3_lo = sb("x3_lo", [P, 2, KC, 2, B], F16)
        hidT = sb("hidT", [P, KC * B])
        outT = sb("outT", [P, KC * B])
        one_o = sb("one_o", [P, KC * B])
        oh = sb("oh", [P, KC * B])
        mem_h = sb("mem_h", [P, KC * B])
        mem = sb("mem", [P, KC * B])
        mT = sb("mT", [P, KC * B])
        om = sb("om", [P, KC * B])
        h3 = sb("h3", [P, 2, KC * B])
        h3_hi = sb("h3_hi", [P, KC * B], F16)
        h3_lo = sb("h3_lo", [P, KC * B], F16)
        x4T = sb("x4T", [P, 2, KC * B])

        banks = [ctx.enter_context(nc.psum_tensor(f"bank{i}", [P, 512], F32)) for i in range(8)]
        pre = banks[0:2]
        tin = banks[2:4]
        tout = banks[4:6]
        setup_ps = banks[6:8]
        mod_ps = banks[4:6]
        R_ps, Z_ps, C_ps, HID_ps, OUT_ps, M_ps, XIN_ps, XOUT_ps = banks
        P_ps = XIN_ps[:, KC * B:]

        def step_at(bank, j):
            return lambda f: bank[:, (2 * f + j % 2) * B:(2 * f + j % 2 + 1) * B]

        def pair_at(bank):
            return lambda f: bank[:, 2 * f * B:2 * (f + 1) * B]

        def alone_at(bank):
            return lambda f: bank[:, f * B:(f + 1) * B]

        def chunked(tile):
            return tile.rearrange("p (c b) -> p c b", b=B)

        x_loaded = sem("x_loaded")
        wx_loaded = sem("wx_loaded")
        cond_loaded = sem("cond_loaded")
        wh_loaded = sem("wh_loaded")
        b0_loaded = sem("b0_loaded")
        w1_loaded = sem("w1_loaded")
        weights_loaded = sem("weights_loaded")
        ident_zero = sem("ident_zero")
        ident_ready = sem("ident_ready")
        pad_ready = sem("pad_ready")
        ones_ready = sem("ones_ready")
        staged = sem("staged")
        x_transposed = sem("x_transposed")
        xT_ready = sem("xT_ready")
        cond_transposed = sem("cond_transposed")
        condT_ready = sem("condT_ready")
        rnn_sum = sem("rnn_sum")
        rnn_h = [sem(f"rnn_h{k}") for k in range(KC)]
        rnn_hi = [sem(f"rnn_hi{k}") for k in range(KC)]
        rnn_lo = [sem(f"rnn_lo{k}") for k in range(KC)]
        rnn_peaks = sem("rnn_peaks")
        rnn_peaks_shared = sem("rnn_peaks_shared")
        rnn_scale = sem("rnn_scale")
        rnn_w_ready = sem("rnn_w_ready")
        rnn_w_split = sem("rnn_w_split")
        h_transposed = sem("h_transposed")
        x1_ready = sem("x1_ready")
        xmax_ready = sem("xmax_ready")
        w1_transposed = sem("w1_transposed")
        w1T_ready = sem("w1T_ready")
        squares_ready = sem("squares_ready")
        norm_sum = sem("norm_sum")
        norm_guess = sem("norm_guess")
        norm_step = sem("norm_step")
        setup_step = sem("setup_step")
        peaks_ready = sem("peaks_ready")
        peaks_shared = sem("peaks_shared")
        scales_ready = sem("scales_ready")
        w_scaled = sem("w_scaled")
        w_hi_ready = sem("w_hi_ready")
        w_lo_ready = sem("w_lo_ready")
        ey_ready = sem("ey_ready")
        e_transposed = sem("e_transposed")
        eyT_ready = sem("eyT_ready")
        mod_sum = sem("mod_sum")
        mod_ready = sem("mod_ready")
        x2_nat = sem("x2_nat")
        staged2 = sem("staged2")
        x2_transposed = sem("x2_transposed")
        x2T_ready = sem("x2T_ready")
        x2_hi_ready = sem("x2_hi_ready")
        x2_split = sem("x2_split")
        r_sum = sem("r_sum")
        z_sum = sem("z_sum")
        c_sum = sem("c_sum")
        p_sum = sem("p_sum")
        r_ready = sem("r_ready")
        z_ready = sem("z_ready")
        c_ready = sem("c_ready")
        p_ready = sem("p_ready")
        rh_ready = sem("rh_ready")
        rh_hi_ready = sem("rh_hi_ready")
        rh_split = sem("rh_split")
        zh_ready = sem("zh_ready")
        keep_ready = sem("keep_ready")
        zc_ready = sem("zc_ready")
        h2_ready = sem("h2_ready")
        h2_hi_ready = sem("h2_hi_ready")
        h2_split_p = sem("h2_split_p")
        h2_next = sem("h2_next")
        x3_ready = sem("x3_ready")
        x3_hi_ready = sem("x3_hi_ready")
        x3_split = sem("x3_split")
        hid_sum = sem("hid_sum")
        out_sum = sem("out_sum")
        mem_sum = sem("mem_sum")
        hid_ready = sem("hid_ready")
        out_ready = sem("out_ready")
        mem_h_ready = sem("mem_h_ready")
        mem_ready = sem("mem_ready")
        m_ready = sem("m_ready")
        oh_ready = sem("oh_ready")
        om_ready = sem("om_ready")
        h3_ready = sem("h3_ready")
        h3_hi_ready = sem("h3_hi_ready")
        h3_split = sem("h3_split")
        x4_ready = sem("x4_ready")
        x4_transposed = sem("x4_transposed")
        x4_nat = sem("x4_nat")
        stored = sem("stored")

        def valid(t, off=0):
            return t is None or 0 <= t + off < T

        def split(t, off=0):
            return t is None or t + off >= UNROLL

        block = ctx.enter_context(nc.Block())

        @block.sync
        def _(sp):
            GC = UNROLL * D
            EARLY = 3
            xv = a["x"].rearrange("b t d -> b (t d)")
            ov = out.rearrange("b t d -> b (t d)")
            sp.dma_start(X[:, 0:GC], xv[:, 0:GC]).then_inc(x_loaded, 16)
            for g in range(1, EARLY):
                sp.wait_ge(x_loaded, 16 * g)
                sp.dma_start(X[:, g * GC:(g + 1) * GC], xv[:, g * GC:(g + 1) * GC]).then_inc(x_loaded, 16)
            for first, name, n in ((Z0, "L2_cond_Wz", 2), (R0, "L2_cond_Wr", 2), (C0, "L2_cond_Wh", 2),
                                   (G0, "L3_cond_w_W", 4), (P0, "L2_cond_Wp", 1), (MX0, "L3_cond_wx_W", 1),
                                   (MH0, "L3_cond_wh_W", 1)):
                src = a[name].rearrange("(c p) n -> p c n", p=P)
                sp.dma_start(W[:, first * CW:(first + n) * CW].rearrange("p (c n) -> p c n", n=src.shape[2]),
                             src).then_inc(weights_loaded, 16)
            for dst, name in ((bz, "L2_cond_bz"), (br, "L2_cond_br"), (bc, "L2_cond_bh"), (bp, "L2_cond_bp"),
                              (bg, "L3_cond_w_b"), (bx, "L3_cond_wx_b"), (bm, "L3_cond_wh_b")):
                sp.dma_start(dst[:, :], a[name].rearrange("(c p) -> p c", p=P),
                             allow_slow_non_contiguous=True).then_inc(weights_loaded, 16)
            with sp.Fori(EARLY, GROUPS) as g:
                sp.wait_ge(x_loaded, g * 16)
                sp.dma_start(X[:, bass.ds(g * GC, GC)], xv[:, bass.ds(g * GC, GC)]).then_inc(x_loaded, 16)
            sp.wait_ge(x4_nat, UNROLL)
            sp.dma_start(ov[:, 0:GC], X[:, 0:GC]).then_inc(stored, 16)
            with sp.Fori(1, GROUPS) as g:
                sp.wait_ge(x4_nat, g * UNROLL + UNROLL)
                sp.dma_start(ov[:, bass.ds(g * GC, GC)], X[:, bass.ds(g * GC, GC)]).then_inc(stored, 16)
            sp.wait_ge(stored, 16 * GROUPS)

        @block.gpsimd
        def _(pool):
            pool.memset(ident[:, :], 0.0).then_inc(ident_zero, 1)
            pool.memset(W[:, (CHUNKS - 1) * CW:], 0.0).then_inc(pad_ready, 1)
            pool.memset(ones[:, :], 1.0).then_inc(ones_ready, 1)
            pool.wait_ge(ident_zero, 1)
            pool.affine_select(out=ident[:, :], in_=ident[:, :], compare_op=ALU.not_equal, fill=1.0,
                               base=0, pattern=[[-1, P]], channel_multiplier=1).then_inc(ident_ready, 1)

            def rnn(t, j, n, pos):
                if valid(t, 4):
                    if t is None or t + 4 >= 2:
                        pool.wait_ge(x_transposed, n(3))
                    if j == 0:
                        if t is None:
                            pool.wait_ge(x_loaded, (pos + 4) * (16 // UNROLL) + 16)
                        else:
                            pool.wait_ge(x_loaded, 16 * ((t + 4) // UNROLL + 1))
                    pool.tensor_tensor(stage[:, j % 2, :], X[:, bass.ds((pos + 4) * D, D)], ones[:, :],
                                       ALU.mult).then_inc(staged, 1)

            pool.wait_ge(ones_ready, 1)
            for t in range(-4, UNROLL):
                rnn(t, t % UNROLL, lambda k, t=t: t + k, t)
                if t == UNROLL - 1:
                    pool.wait_ge(condT_ready, 1)
                    pool.tensor_tensor(condT2[:, :, :], condT[:, :, :], condT[:, :, :], ALU.mult)
                    pool.wait_ge(w1T_ready, 1)
                    pool.tensor_tensor(w1T2[:, :, :], w1T[:, :, :], w1T[:, :, :], ALU.mult
                                       ).then_inc(squares_ready, 1)
                if t == -1:
                    pool.wait_ge(rnn_peaks, 1)
                    pool.partition_all_reduce(peak0_all[:, :], peak0[:, :], P, bass.bass_isa.ReduceOp.max
                                              ).then_inc(rnn_peaks_shared, 1)
            with pool.Fori(1, GROUPS - 1) as i:
                base = Count(pool, i * UNROLL)
                for j in range(UNROLL):
                    rnn(None, j, lambda k, j=j: base(j + k), i * UNROLL + j)
            def share_peaks(nth, first, end):
                pool.wait_ge(peaks_ready, nth)
                pool.partition_all_reduce(peak_all[:, first:end], peak[:, first:end], P,
                                          bass.bass_isa.ReduceOp.max).then_inc(peaks_shared, 1)

            pool.wait_ge(norm_guess, 1)
            for nth in range(REFINEMENTS):
                if nth:
                    pool.wait_ge(norm_step, 4 * nth)
                pool.tensor_tensor(norm_q[:, :], norm_r[:, :], norm_r[:, :], ALU.mult).then_inc(norm_step, 1)
                pool.wait_ge(norm_step, 4 * nth + 1)
                pool.tensor_tensor(norm_q[:, :], norm_q[:, :], norm_v[:, :], ALU.mult).then_inc(norm_step, 1)
                pool.wait_ge(norm_step, 4 * nth + 2)
                pool.tensor_scalar(norm_q[:, :], norm_q[:, :], -0.5, 1.5, ALU.mult, ALU.add).then_inc(norm_step, 1)
                pool.wait_ge(norm_step, 4 * nth + 3)
                pool.tensor_tensor(norm_r[:, :], norm_r[:, :], norm_q[:, :], ALU.mult).then_inc(norm_step, 1)
            share_peaks(1, 0, CHUNKS)

            def modulate(t, j, n, pos):
                if valid(t, 2):
                    if t is None or t >= 0:
                        pool.wait_ge(e_transposed, n(1))
                    pool.tensor_tensor(ey[:, j % 2, :], X_il[:, :, bass.ds(pos + 2, 1)], cond[:, :],
                                       ALU.mult).then_inc(ey_ready, 1)

            pool.wait_ge(x1_ready, T)
            pool.wait_ge(cond_loaded, 16)
            for t in range(-2, UNROLL):
                modulate(t, t % UNROLL, lambda k, t=t: t + k, t)
            share_peaks(2, CHUNKS, CHUNKS + 2)
            with pool.Fori(1, GROUPS - 1) as i:
                base = Count(pool, i * UNROLL)
                for j in range(UNROLL):
                    modulate(None, j, lambda k, j=j: base(j + k), i * UNROLL + j)
            for t in range(T - UNROLL, T):
                modulate(t, t % UNROLL, lambda k, t=t: t + k, t)

            def gates(t, j, n, pos):
                if valid(t):
                    h = h2p[:, :] if j == 0 and (t is None or t > 0) else h2[:, (j + 1) % 2, :]
                    pool.wait_ge(z_ready, n(1))
                    pool.tensor_tensor(zh[:, :], zT[:, :], h, ALU.mult).then_inc(zh_ready, 1)
                    pool.wait_ge(zh_ready, n(1))
                    pool.tensor_tensor(keep[:, :], h, zh[:, :], ALU.subtract).then_inc(keep_ready, 1)
                if valid(t, -3):
                    pool.wait_ge(h3_ready, n(-2))
                    if t is None or t >= 5:
                        pool.wait_ge(x4_transposed, n(-4))
                    pool.tensor_tensor(x4T[:, (j + 1) % 2, :], x3T[:, (j + 1) % UNROLL, :], h3[:, (j + 1) % 2, :],
                                       ALU.add).then_inc(x4_ready, 1)
                if valid(t):
                    pool.wait_ge(h2_ready, n(1))
                    pool.tensor_tensor(x3T[:, j, :], x2T[:, j, :], h2[:, j % 2, :], ALU.add
                                       ).then_inc(x3_ready, 1)
                    pool.wait_ge(x3_hi_ready, n(1))
                    pool.tensor_tensor(x3_lo[:, j // 2, :, j % 2, :], chunked(x3T[:, j, :]),
                                       x3_hi[:, j // 2, :, j % 2, :], ALU.subtract).then_inc(x3_split, 1)
                if valid(t, 4):
                    if t is None or t >= 2:
                        pool.wait_ge(x2_transposed, n(3))
                    pool.tensor_tensor(stage[:, j % 2, :], X[:, bass.ds((pos + 4) * D, D)], ones[:, :],
                                       ALU.mult).then_inc(staged2, 1)
                if valid(t, -2):
                    pool.wait_ge(out_ready, n(-1))
                    pool.tensor_tensor(oh[:, :], outT[:, :], h3[:, (j + 1) % 2, :], ALU.mult)
                    pool.tensor_scalar(one_o[:, :], outT[:, :], -1.0, 1.0, ALU.mult, ALU.add
                                       ).then_inc(oh_ready, 1)

            pool.wait_ge(x2_nat, L)
            for t in range(UNROLL):
                gates(t, t % UNROLL, lambda k, t=t: t + k, t)
            with pool.Fori(1, GROUPS - 1) as i:
                base = Count(pool, i * UNROLL)
                for j in range(UNROLL):
                    gates(None, j, lambda k, j=j: base(j + k), i * UNROLL + j)
            for t in range(T - UNROLL, T + 4):
                gates(t, t % UNROLL, lambda k, t=t: t + k, t)

        @block.scalar
        def _(act):
            act.dma_start(wx0[:, :, :], a["L0_cond_Wx"].rearrange("(c p) n -> p c n", p=P)).then_inc(wx_loaded, 16)
            act.dma_start(cond[:, :], a["cond_1024"]).then_inc(cond_loaded, 16)
            act.dma_start(wh0[:, :, :], a["L0_cond_Wh"].rearrange("(c p) n -> p c n", p=P)).then_inc(wh_loaded, 16)
            act.dma_start(b0[:, :], a["L0_cond_b"].rearrange("(c p) -> p c", p=P),
                          allow_slow_non_contiguous=True).then_inc(b0_loaded, 16)
            act.dma_start(w1[:, :, :], a["L1_cond_weight"].rearrange("e (c p) i f -> p c (e i f)", p=P)
                          ).then_inc(w1_loaded, 16)
            act.wait_ge(ones_ready, 1)
            nc.scalar.activation(warm[:, :], ones[:, 0:1], ACT.Sigmoid)

            def rnn(t, j, n, pos):
                if valid(t):
                    act.wait_ge(rnn_sum, n(1))
                    for f in range(KC):
                        nc.scalar.activation(h0T[:, j % 2, f, :], step_at(pre[j // 2], j)(f), ACT.Tanh,
                                             bias=b0[:, f:f + 1], scale=undo0[:, :] if split(t) else 1.0
                                             ).then_inc(rnn_h[f], 1)
                if split(t, 1) and valid(t, 1):
                    for f in range(KC):
                        act.wait_ge(rnn_h[f], n(1))
                        nc.scalar.activation(h0_hi[:, f, :], h0T[:, j % 2, f, :], ACT.Copy, scale=H_SCALE
                                             ).then_inc(rnn_hi[f], 1)

            act.wait_ge(b0_loaded, 16)
            for t in range(UNROLL):
                rnn(t, t % UNROLL, lambda k, t=t: t + k, t)
                if t == 0:
                    act.wait_ge(rnn_scale, 1)
                    nc.scalar.activation(wx0_s[:, :, :], wx0[:, :, :], ACT.Copy, scale=scale0[:, :]
                                         ).then_inc(rnn_w_ready, 1)
                if t == UNROLL - 3:
                    act.wait_ge(w1_transposed, 1)
                    nc.scalar.activation(w1T[:, :, :].rearrange("p c n -> p (c n)"), setup_ps[1][:, 0:CW], ACT.Copy
                                         ).then_inc(w1T_ready, 1)
                if t == UNROLL - 2:
                    nc.scalar.activation(wh0_hi[:, :, :], wh0[:, :, :], ACT.Copy, scale=scale[:, S0:S0 + 1]
                                         ).then_inc(rnn_w_ready, 1)
            with act.Fori(1, GROUPS - 1) as i:
                base = Count(act, i * UNROLL)
                for j in range(UNROLL):
                    rnn(None, j, lambda k, j=j: base(j + k), i * UNROLL + j)
            for t in range(T - UNROLL, T):
                rnn(t, t % UNROLL, lambda k, t=t: t + k, t)

            def modulate(t, j, n, pos):
                if valid(t, 2):
                    act.wait_ge(e_transposed, n(3))
                    nc.scalar.activation(eyT[:, j % 2, :, :].rearrange("p c b -> p (c b)"),
                                         tin[j % 2][:, 0:KC * B], ACT.Copy).then_inc(eyT_ready, 1)

            for t in range(-2, UNROLL):
                modulate(t, t % UNROLL, lambda k, t=t: t + k, t)
            act.wait_ge(scales_ready, 1)
            act.wait_ge(weights_loaded, 16 * 14)
            with act.Fori(1, GROUPS - 1) as i:
                base = Count(act, i * UNROLL)
                done = act.snap(i)
                for j in range(UNROLL):
                    modulate(None, j, lambda k, j=j: base(j + k), i * UNROLL + j)
                    chunk = W[:, bass.ds(i * CW - CW, CW)]
                    if j == 0:
                        nc.scalar.activation(chunk, chunk, ACT.Copy,
                                             scale=chunk_scale[:, bass.ds(i - 1, 1)]).then_inc(w_scaled, 1)
                    if j == 2:
                        act.wait_ge(w_scaled, done)
                        nc.scalar.activation(W_hi[:, bass.ds(i * CW - CW, CW)], chunk, ACT.Copy
                                             ).then_inc(w_hi_ready, 1)
            for t in range(T - UNROLL, T):
                modulate(t, t % UNROLL, lambda k, t=t: t + k, t)

            act.wait_ge(scales_ready, 2)

            def gate(dst, src, func, column, b, ready):
                for f in range(KC):
                    last = nc.scalar.activation(dst[:, f * B:(f + 1) * B], src(f), func,
                                                bias=b[:, f:f + 1], scale=undo_sum[:, column:column + 1])
                last.then_inc(ready, 1)

            def candidate(steps):
                act.wait_ge(mem_ready, steps)
                gate(mT, alone_at(mem), ACT.Tanh, SM, bx, m_ready)

            def gates(t, j, n, pos):
                if valid(t):
                    act.wait_ge(r_sum, n(1))
                    gate(rT, step_at(R_ps, j), ACT.Sigmoid, SR, br, r_ready)
                if j % 2 and valid(t, -3):
                    candidate(n(-2))
                if valid(t):
                    act.wait_ge(z_sum, n(1))
                    gate(zT, step_at(Z_ps, j), ACT.Sigmoid, SZ, bz, z_ready)
                if valid(t, -4):
                    act.wait_ge(x4_transposed, n(-3))
                    nc.scalar.activation(X[:, bass.ds((pos - 4) * D, D)], XOUT_ps[:, 0:D], ACT.Copy,
                                         scale=undo[:, SA:SA + 1]).then_inc(x4_nat, 1)
                if valid(t):
                    act.wait_ge(c_sum, n(1))
                    gate(cT, step_at(C_ps, j), ACT.Tanh, SC, bc, c_ready)
                if valid(t, 3):
                    act.wait_ge(x2_transposed, n(4))
                    if t is None or t >= 1:
                        act.wait_ge(x3_ready, n(0))
                    nc.scalar.activation(x2T[:, (j + 3) % UNROLL, :], XIN_ps[:, 0:KC * B], ACT.Copy,
                                         scale=scale[:, SA:SA + 1]).then_inc(x2T_ready, 1)
                if valid(t, -2):
                    act.wait_ge(hid_sum, n(-1))
                    gate(hidT, step_at(HID_ps, j), ACT.Sigmoid, SG, bg, hid_ready)
                    act.wait_ge(out_sum, n(-1))
                    gate(outT, step_at(OUT_ps, j), ACT.Sigmoid, SG, bg[:, KC:], out_ready)
                if valid(t) and j == UNROLL - 1 and (t is None or t < T - 1):
                    act.wait_ge(p_sum, (t + 1) // UNROLL if t is not None else known["nth"])
                    gate(pT, alone_at(P_ps), ACT.Tanh, SP, bp, p_ready)
                if j % 2 and valid(t, -2):
                    candidate(n(-1))

            known = {}
            for t in range(-3, UNROLL):
                gates(t, t % UNROLL, lambda k, t=t: t + k, t)
            with act.Fori(1, GROUPS - 1) as i:
                base = Count(act, i * UNROLL)
                known["nth"] = act.snap(i + 1)
                for j in range(UNROLL):
                    gates(None, j, lambda k, j=j: base(j + k), i * UNROLL + j)
            for t in range(T - UNROLL, T + 4):
                gates(t, t % UNROLL, lambda k, t=t: t + k, t)

        @block.vector
        def _(dve):
            def rnn(t, j, n, pos):
                if valid(t, 4):
                    dve.wait_ge(x_transposed, n(5))
                    nc.vector.tensor_copy(xT[:, j // 2, :, j % 2, :], chunked(tin[j % 2][:, 0:KC * B])
                                          ).then_inc(xT_ready, 1)
                if split(t, 1) and valid(t, 1):
                    for f in range(KC):
                        dve.wait_ge(rnn_hi[f], n(-UNROLL + 2))
                        nc.vector.scalar_tensor_tensor(h0_lo[:, f, :], h0T[:, j % 2, f, :], H_SCALE,
                                                       h0_hi[:, f, :], ALU.mult, ALU.subtract
                                                       ).then_inc(rnn_lo[f], 1)
                if t == -3:
                    dve.wait_ge(cond_transposed, 1)
                    nc.vector.tensor_copy(condT[:, :, :].rearrange("p c b -> p (c b)"), setup_ps[0][:, 0:KC * B]
                                          ).then_inc(condT_ready, 1)
                if valid(t, -1):
                    dve.wait_ge(h_transposed, n(0))
                    x1 = X[:, bass.ds((pos - 1) * D, D)]
                    nc.vector.tensor_tensor(x1, tout[(j + 1) % 2][:, 0:D], x1, ALU.add).then_inc(x1_ready, 1)
                if valid(t, -2):
                    dve.wait_ge(x1_ready, n(-1))
                    nc.vector.tensor_reduce(xmax[:, bass.ds(pos - 2, 1)], X[:, bass.ds((pos - 2) * D, D)],
                                            AX, ALU.max, apply_absolute_value=True).then_inc(xmax_ready, 1)

            chain = [0]

            def link(ins):
                chain[0] += 1
                ins.then_inc(setup_step, 1)
                dve.wait_ge(setup_step, chain[0])

            def flat(tile):
                return tile[:, :, :].rearrange("p c n -> p (c n)")

            def first_guess():
                dve.wait_ge(norm_sum, 1)
                link(nc.vector.tensor_scalar(norm_v[:, :], setup_ps[0][:, 0:D], 1.0 / D, 1e-8, ALU.mult, ALU.add))
                nc.vector.tensor_scalar(norm_r[:, :].bitcast(I32), norm_v[:, :].bitcast(I32), -0.5,
                                        float(0x5F3759DF), ALU.mult, ALU.add).then_inc(norm_guess, 1)

            def widest(column, first, count):
                return nc.vector.tensor_reduce(top[:, column:column + 1], peak_all[:, first:first + count], AX,
                                               ALU.max)

            def power_of_two(first, end, least, e):
                at = slice(first, end)
                link(nc.vector.tensor_scalar(top[:, at], top[:, at], least, None, ALU.max))
                link(nc.vector.tensor_scalar(power[:, at].bitcast(I32), top[:, at].bitcast(I32), 0x7F800000, None,
                                             ALU.bitwise_and))
                nc.vector.tensor_scalar(scale[:, at].bitcast(I32), power[:, at].bitcast(I32), -1.0,
                                        float((254 + e) << 23), ALU.mult, ALU.add)
                link(nc.vector.tensor_scalar(undo[:, at], power[:, at], 2.0 ** -e, None, ALU.mult))

            def weight_scales():
                dve.wait_ge(peaks_shared, 1)
                for column, first, count in ((SZ, Z0, 2), (SR, R0, 2), (SC, C0, 2), (SG, G0, 4), (SP, P0, 1)):
                    widest(column, first, count)
                link(widest(SM, MX0, 2))
                power_of_two(SZ, SA, 2.0 ** -100, W_EXP)
                for c0, count, column in ((Z0, 2, SZ), (R0, 2, SR), (C0, 2, SC), (G0, 4, SG), (P0, 1, SP),
                                          (MX0, 3, SM)):
                    last = nc.vector.tensor_copy(chunk_scale[:, c0:c0 + count],
                                                 scale[:, column:column + 1].to_broadcast([P, count]))
                last.then_inc(scales_ready, 1)

            def activation_scale():
                dve.wait_ge(peaks_shared, 2)
                link(widest(SA, XMAX, 2))
                power_of_two(SA, NS, 1.0, A_EXP)
                nc.vector.tensor_scalar(undo_sum[:, :], undo[:, :], undo[:, SA:SA + 1], None, ALU.mult)
                link(nc.vector.tensor_scalar(scale_m[:, :], scale[:, SM:SM + 1], scale[:, SA:SA + 1], None,
                                             ALU.mult))
                nc.vector.tensor_scalar(bm_s[:, :], bm[:, :], scale_m[:, :], None, ALU.mult).then_inc(scales_ready, 1)

            def rnn_weight_peak(nth, w, loaded):
                dve.wait_ge(loaded, 16)
                return nc.vector.tensor_reduce(peak0[:, nth:nth + 1], flat(w), AX, ALU.max,
                                               apply_absolute_value=True)

            def rnn_scales():
                dve.wait_ge(rnn_peaks_shared, 1)
                link(nc.vector.tensor_reduce(top[:, S0:S0 + 1], peak0_all[:, :], AX, ALU.max))
                power_of_two(S0, S0 + 1, 2.0 ** -60, W_EXP)
                nc.vector.tensor_scalar(undo0[:, :], undo[:, S0:S0 + 1], 1 / H_SCALE, None, ALU.mult)
                nc.vector.tensor_scalar(scale0[:, :], scale[:, S0:S0 + 1], H_SCALE, None, ALU.mult
                                        ).then_inc(rnn_scale, 1)

            for t in range(-4, UNROLL):
                rnn(t, t % UNROLL, lambda k, t=t: t + k, t)
                if t == -3:
                    rnn_weight_peak(0, wx0, wx_loaded)
                    rnn_weight_peak(1, wh0, wh_loaded).then_inc(rnn_peaks, 1)
                if t == -1:
                    rnn_scales()
                if t == 2:
                    dve.wait_ge(rnn_w_ready, 2)
                    nc.vector.scalar_tensor_tensor(flat(wh0_lo), flat(wh0), scale[:, S0:S0 + 1], flat(wh0_hi),
                                                   ALU.mult, ALU.subtract).then_inc(rnn_w_split, 1)
            first_guess()

            dve.wait_ge(pad_ready, 1)
            with dve.Fori(1, GROUPS - 1) as i:
                base = Count(dve, i * UNROLL)
                for j in range(UNROLL):
                    rnn(None, j, lambda k, j=j: base(j + k), i * UNROLL + j)
                dve.wait_ge(weights_loaded, 16 * 14)
                nc.vector.tensor_reduce(peak[:, bass.ds(i - 1, 1)], W[:, bass.ds(i * CW - CW, CW)], AX, ALU.max,
                                        apply_absolute_value=True)
            nc.vector.tensor_reduce(peak[:, HMAX:HMAX + 1], cond[:, :], AX, ALU.max, apply_absolute_value=True
                                    ).then_inc(peaks_ready, 1)
            for t in range(T - UNROLL, T + 2):
                rnn(t, t % UNROLL, lambda k, t=t: t + k, t)
                if t == T:
                    weight_scales()
            dve.wait_ge(xmax_ready, T)
            nc.vector.tensor_reduce(peak[:, XMAX:XMAX + 1], xmax[:, :], AX, ALU.max).then_inc(peaks_ready, 1)
            dve.wait_ge(norm_step, 4 * REFINEMENTS)
            link(nc.vector.tensor_scalar(gain[:, :], norm_r[:, :], float(D) ** -0.5, None, ALU.mult))

            def modulate(t, j, n, pos):
                if valid(t):
                    dve.wait_ge(mod_sum, n(1))
                    if t is None or t >= 2:
                        dve.wait_ge(x2_nat, n(-1))
                    nc.vector.tensor_tensor(mod[:, j % 2, :], mod_ps[j % 2][:, 0:D], gain[:, :], ALU.mult
                                            ).then_inc(mod_ready, 1)
                if valid(t, -1):
                    dve.wait_ge(mod_ready, n(0))
                    x2 = X_il[:, :, bass.ds(pos - 1, 1)]
                    nc.vector.tensor_tensor(x2, mod[:, (j + 1) % 2, :], x2, ALU.add).then_inc(x2_nat, 1)

            for t in range(UNROLL):
                modulate(t, t % UNROLL, lambda k, t=t: t + k, t)
            activation_scale()
            with dve.Fori(1, GROUPS - 1) as i:
                base = Count(dve, i * UNROLL)
                chunks = dve.snap(i)
                for j in range(UNROLL):
                    modulate(None, j, lambda k, j=j: base(j + k), i * UNROLL + j)
                dve.wait_ge(w_hi_ready, chunks)
                nc.vector.tensor_tensor(W_lo[:, bass.ds(i * CW - CW, CW)], W[:, bass.ds(i * CW - CW, CW)],
                                        W_hi[:, bass.ds(i * CW - CW, CW)], ALU.subtract).then_inc(w_lo_ready, 1)
            for t in range(T - UNROLL, T + 1):
                modulate(t, t % UNROLL, lambda k, t=t: t + k, t)

            for dst in (h2, h3):
                last = nc.vector.tensor_scalar(dst[:, 1, :], condT[:, :, :].rearrange("p c b -> p (c b)"),
                                               scale[:, SA:SA + 1], None, ALU.mult)
            link(last)
            nc.vector.tensor_copy(h2_hi[:, :], h2[:, 1, :])
            nc.vector.tensor_copy(h3_hi[:, :], h3[:, 1, :]).then_inc(h3_hi_ready, 1)
            dve.wait_ge(h3_hi_ready, 1)
            nc.vector.tensor_tensor(h2_lo[:, :], h2[:, 1, :], h2_hi[:, :], ALU.subtract).then_inc(h2_next, 1)
            nc.vector.tensor_tensor(h3_lo[:, :], h3[:, 1, :], h3_hi[:, :], ALU.subtract).then_inc(h3_split, 1)

            def reset_state(t, j, n):
                if valid(t):
                    h = h2p[:, :] if j == 0 and (t is None or t > 0) else h2[:, (j + 1) % 2, :]
                    dve.wait_ge(r_ready, n(1))
                    nc.vector.tensor_tensor(rh[:, :], rT[:, :], h, ALU.mult).then_inc(rh_ready, 1)

            def reset_state_hi(t, n):
                if valid(t):
                    dve.wait_ge(rh_ready, n(1))
                    nc.vector.tensor_copy(rh_hi[:, :], rh[:, :]).then_inc(rh_hi_ready, 1)

            def reset_state_lo(t, n):
                if valid(t):
                    dve.wait_ge(rh_hi_ready, n(1))
                    nc.vector.tensor_tensor(rh_lo[:, :], rh[:, :], rh_hi[:, :], ALU.subtract
                                            ).then_inc(rh_split, 1)

            def input_hi(t, j, n, off):
                if valid(t, off):
                    dve.wait_ge(x2T_ready, n(off + 1))
                    if t is None or t >= 0:
                        dve.wait_ge(r_sum, n(1))
                    nc.vector.tensor_copy(x2_hi[:, :, off % 2, :], chunked(x2T[:, (j + off) % UNROLL, :])
                                          ).then_inc(x2_hi_ready, 1)

            def input_lo(t, j, n, off):
                if valid(t, off):
                    dve.wait_ge(x2_hi_ready, n(off + 1))
                    nc.vector.tensor_tensor(x2_lo[:, :, off % 2, :], chunked(x2T[:, (j + off) % UNROLL, :]),
                                            x2_hi[:, :, off % 2, :], ALU.subtract).then_inc(x2_split, 1)

            def new_part(t, n):
                if valid(t, -3):
                    dve.wait_ge(m_ready, n(-2))
                    dve.wait_ge(oh_ready, n(-2))
                    nc.vector.scalar_tensor_tensor(om[:, :], mT[:, :], scale[:, SA:SA + 1], one_o[:, :],
                                                   ALU.mult, ALU.mult).then_inc(om_ready, 1)

            def state(t, j, n):
                if valid(t, -3):
                    dve.wait_ge(om_ready, n(-2))
                    nc.vector.tensor_tensor(h3[:, (j + 1) % 2, :], om[:, :], oh[:, :], ALU.add
                                            ).then_inc(h3_ready, 1)

            def state_hi(t, j, n):
                if valid(t, -3):
                    dve.wait_ge(h3_ready, n(-2))
                    nc.vector.tensor_copy(h3_hi[:, :], h3[:, (j + 1) % 2, :]).then_inc(h3_hi_ready, 1)

            def state_lo(t, j, n):
                if valid(t, -3):
                    dve.wait_ge(h3_hi_ready, n(-1))
                    nc.vector.tensor_tensor(h3_lo[:, :], h3[:, (j + 1) % 2, :], h3_hi[:, :], ALU.subtract
                                            ).then_inc(h3_split, 1)

            def gates(t, j, n, pos):
                if j % 2 == 0:
                    new_part(t, n)
                    state(t, j, n)
                    state_hi(t, j, n)
                    state_lo(t, j, n)
                    reset_state(t, j, n)
                    reset_state_hi(t, n)
                    input_hi(t, j, n, 2)
                    reset_state_lo(t, n)
                    input_lo(t, j, n, 2)
                else:
                    reset_state(t, j, n)
                    reset_state_hi(t, n)
                    new_part(t, n)
                    reset_state_lo(t, n)
                    state(t, j, n)
                    state_hi(t, j, n)
                    state_lo(t, j, n)
                if valid(t):
                    dve.wait_ge(c_ready, n(1))
                    nc.vector.scalar_tensor_tensor(zc[:, :], cT[:, :], scale[:, SA:SA + 1], zT[:, :],
                                                   ALU.mult, ALU.mult).then_inc(zc_ready, 1)
                    dve.wait_ge(keep_ready, n(1))
                    dve.wait_ge(zc_ready, n(1))
                    nc.vector.tensor_tensor(h2[:, j % 2, :], zc[:, :], keep[:, :], ALU.add).then_inc(h2_ready, 1)
                    if t is None or t < T - 1:
                        dve.wait_ge(h2_ready, n(1))
                        nc.vector.tensor_copy(h2_hi[:, :], h2[:, j % 2, :]).then_inc(h2_hi_ready, 1)
                        dve.wait_ge(h2_hi_ready, pairs(t, j, pos))
                        nc.vector.tensor_tensor(h2_lo[:, :], h2[:, j % 2, :], h2_hi[:, :], ALU.subtract
                                                ).then_inc(h2_split_p if j == UNROLL - 1 else h2_next, 1)
                if valid(t):
                    dve.wait_ge(x3_ready, n(1))
                    nc.vector.tensor_copy(x3_hi[:, j // 2, :, j % 2, :], chunked(x3T[:, j, :])).then_inc(x3_hi_ready, 1)
                if valid(t, -2):
                    dve.wait_ge(mem_sum, n(-1))
                    dve.wait_ge(hid_ready, n(-1))
                    for f in range(KC):
                        at = slice(f * B, (f + 1) * B)
                        last = nc.vector.scalar_tensor_tensor(mem_h[:, at], M_ps[:, KC * B + f * B:KC * B + (f + 1) * B],
                                                              bm_s[:, f:f + 1], hidT[:, at], ALU.add, ALU.mult)
                    last.then_inc(mem_h_ready, 1)
                    dve.wait_ge(mem_h_ready, n(-1))
                    nc.vector.tensor_tensor(mem[:, :], M_ps[:, 0:KC * B], mem_h[:, :], ALU.add
                                            ).then_inc(mem_ready, 1)
                if j % 2 == 0:
                    input_hi(t, j, n, 3)
                    input_lo(t, j, n, 3)
                if valid(t) and j == UNROLL - 1 and (t is None or t < T - 1):
                    dve.wait_ge(p_ready, nth(t, pos))
                    nc.vector.tensor_scalar(h2_hi[:, :], pT[:, :], scale[:, SA:SA + 1], None, ALU.mult
                                            ).then_inc(h2_hi_ready, 1)
                    nc.vector.tensor_scalar(h2p[:, :], pT[:, :], scale[:, SA:SA + 1], None, ALU.mult)
                    dve.wait_ge(h2_hi_ready, pairs(t, j, pos, 1))
                    nc.vector.scalar_tensor_tensor(h2_lo[:, :], pT[:, :], scale[:, SA:SA + 1], h2_hi[:, :],
                                                   ALU.mult, ALU.subtract).then_inc(h2_next, 1)

            known = {}

            def nth(t, pos):
                return (t + 1) // UNROLL if t is not None else known["nth"]

            def pairs(t, j, pos, more=0):
                if t is not None:
                    return t // UNROLL * (UNROLL + 1) + j + 1 + more
                if j + more not in known:
                    known[j + more] = dve.snap(known["i"] * (UNROLL + 1) + (j + more + 1))
                return known[j + more]

            for t in range(-2, UNROLL):
                gates(t, t % UNROLL, lambda k, t=t: t + k, t)
            with dve.Fori(1, GROUPS - 1) as i:
                base = Count(dve, i * UNROLL)
                known.clear()
                known["i"] = i
                known["nth"] = dve.snap(i + 1)
                for j in range(UNROLL):
                    gates(None, j, lambda k, j=j: base(j + k), i * UNROLL + j)
            for t in range(T - UNROLL, T + 4):
                gates(t, t % UNROLL, lambda k, t=t: t + k, t)

        @block.tensor
        def _(pe):
            def mm(dst, lhsT, rhs, start=False):
                return nc.tensor.matmul(dst, lhsT, rhs, start=start, stop=True, skip_group_check=True)

            def transposed(dst, src):
                for c in range(KC):
                    last = nc.tensor.transpose(dst[:, c * P:(c + 1) * P], src[:, c * P:(c + 1) * P], ident[:, :])
                return last

            def keep_warm(count, bank):
                for _ in range(count):
                    nc.tensor.transpose(bank[:, 0:P], ident[:, :], ident[:, :])

            def rnn(t, j, n, pos):
                sums = step_at(pre[j // 2], j)
                if valid(t) and split(t):
                    for k in range(KC):
                        pe.wait_ge(rnn_hi[k], n(-UNROLL + 1))
                        for f in range(KC):
                            for w in (wh0_hi, wh0_lo):
                                mm(sums(f), w[:, k, f * P:(f + 1) * P], h0_hi[:, k, :])
                    for k in range(KC):
                        pe.wait_ge(rnn_lo[k], n(-UNROLL + 1))
                        for f in range(KC):
                            last = mm(sums(f), wh0_hi[:, k, f * P:(f + 1) * P],
                                      h0_lo[:, k, :])
                    last.then_inc(rnn_sum, 1)
                elif valid(t):
                    for k in range(KC):
                        if t == 0:
                            pe.wait_ge(condT_ready, 1)
                            pe.wait_ge(wh_loaded, 16)
                            h = condT[:, k, :]
                        else:
                            pe.wait_ge(rnn_h[k], n(0))
                            if j % 2 == 1:
                                pe.wait_ge(rnn_h[1], n(0))
                            h = h0T[:, (j + 1) % 2, k, :]
                        for f in range(KC):
                            last = mm(sums(f), wh0[:, k, f * P:(f + 1) * P], h)
                    last.then_inc(rnn_sum, 1)
                if valid(t, 4):
                    pe.wait_ge(staged, n(5))
                    if t is None or t >= -2:
                        pe.wait_ge(xT_ready, n(3))
                    transposed(tin[j % 2], stage[:, j % 2, :]).then_inc(x_transposed, 1)
                f, ahead = j % 2, 2 - j % 2
                if valid(t, ahead) and (t is None or t >= -2):
                    if t == -2:
                        pe.wait_ge(wx_loaded, 16)
                    if t == UNROLL - 2:
                        pe.wait_ge(rnn_w_ready, 1)
                    pe.wait_ge(xT_ready, n(ahead + 2))
                    wx = wx0_s if split(t, ahead) else wx0
                    for k in range(KC):
                        mm(pair_at(pre[(j // 2 + 1) % 2])(f), wx[:, k, f * P:(f + 1) * P],
                           xT[:, (j // 2 + 1) % 2, k, :, :].rearrange("p s b -> p (s b)"),
                           start=(k == 0 and f == 0))
                if t == -3:
                    pe.wait_ge(cond_loaded, 16)
                    transposed(setup_ps[0], cond).then_inc(cond_transposed, 1)
                if valid(t, -1):
                    if t == T:
                        for k in range(KC):
                            pe.wait_ge(rnn_h[k], T)
                    if t is None or t >= 3:
                        pe.wait_ge(x1_ready, n(-2))
                    transposed(tout[(j + 1) % 2], h0T[:, (j + 1) % 2, :, :].rearrange("p c b -> p (c b)")
                               ).then_inc(h_transposed, 1)

            pe.wait_ge(ident_ready, 1)
            keep_warm(12, setup_ps[0])
            for t in range(-4, UNROLL):
                rnn(t, t % UNROLL, lambda k, t=t: t + k, t)
                if t == 1:
                    pe.wait_ge(w1_loaded, 16)
                    for c in range(KC):
                        for o in range(KC):
                            last = nc.tensor.transpose(setup_ps[1][:, c * D + o * P:c * D + (o + 1) * P],
                                                       w1[:, o, c * P:(c + 1) * P], ident[:, :])
                    last.then_inc(w1_transposed, 1)
            pe.wait_ge(rnn_w_split, 1)
            pe.wait_ge(squares_ready, 1)
            for k in range(KC):
                last = mm(setup_ps[0][:, 0:D], condT2[:, k, :], w1T2[:, k, :], start=(k == 0))
            last.then_inc(norm_sum, 1)

            with pe.Fori(1, GROUPS - 1) as i:
                base = Count(pe, i * UNROLL)
                for j in range(UNROLL):
                    rnn(None, j, lambda k, j=j: base(j + k), i * UNROLL + j)
            for t in range(T - UNROLL, T + 1):
                rnn(t, t % UNROLL, lambda k, t=t: t + k, t)

            keep_warm(24, setup_ps[0])

            def modulate(t, j, n, pos):
                if valid(t):
                    pe.wait_ge(eyT_ready, n(1))
                    if t is None or t >= 2:
                        pe.wait_ge(mod_ready, n(-1))
                    for k in range(KC):
                        last = mm(mod_ps[j % 2][:, 0:D], eyT[:, j % 2, k, :], w1T[:, k, :], start=(k == 0))
                    last.then_inc(mod_sum, 1)
                if valid(t, 2):
                    pe.wait_ge(ey_ready, n(3))
                    if t is None or t >= 0:
                        pe.wait_ge(eyT_ready, n(1))
                    transposed(tin[j % 2], ey[:, j % 2, :]).then_inc(e_transposed, 1)

            for t in range(-2, UNROLL):
                modulate(t, t % UNROLL, lambda k, t=t: t + k, t)
            with pe.Fori(1, GROUPS - 1) as i:
                base = Count(pe, i * UNROLL)
                for j in range(UNROLL):
                    modulate(None, j, lambda k, j=j: base(j + k), i * UNROLL + j)
            for t in range(T - UNROLL, T):
                modulate(t, t % UNROLL, lambda k, t=t: t + k, t)

            def flat(tile):
                return lambda k: tile[:, k, :, :].rearrange("p s b -> p (s b)")

            def product(dst, w_at, x_hi, x_lo, begins=False):
                for k in range(KC):
                    for f in range(KC):
                        c = w_at(k, f)
                        for w, x in ((W_hi, x_hi), (W_hi, x_lo), (W_lo, x_hi)):
                            last = mm(dst(f), w[:, c:c + P], x(k), begins)
                            begins = False
                return last

            def high_part(dst, w_at, x_hi):
                for k in range(KC):
                    for f in range(KC):
                        for w in (W_hi, W_lo):
                            mm(dst(f), w[:, w_at(k, f):w_at(k, f) + P], x_hi(k))

            def low_part(dst, w_at, x_lo):
                for k in range(KC):
                    for f in range(KC):
                        last = mm(dst(f), W_hi[:, w_at(k, f):w_at(k, f) + P], x_lo(k))
                return last

            def block_at(chunk):
                return lambda k, f: chunk * CW + k * D + f * P

            def fused_at(half, part):
                return lambda k, f: (G0 + 2 * half + k) * CW + part * D + f * P

            h2_pair = alone_at(h2_hi), alone_at(h2_lo)
            h3_pair = alone_at(h3_hi), alone_at(h3_lo)

            def memory_of_x(t, j, n):
                pair, step = (j + 2) // 2 % 2, j % 2
                pe.wait_ge(x3_split, n(-1))
                if t is None or t >= 3:
                    pe.wait_ge(mem_ready, n(-2))
                product(alone_at(M_ps), block_at(MX0), lambda k: x3_hi[:, pair, k, step, :],
                        lambda k: x3_lo[:, pair, k, step, :], True)

            def last_fused_of_x(step, bank, part):
                pair = (T - 2) // 2 % 2
                pe.wait_ge(x3_split, T - 1 + step)
                product(step_at(bank, step), fused_at(0, part), lambda k: x3_hi[:, pair, k, step, :],
                        lambda k: x3_lo[:, pair, k, step, :], step == 0)

            def fused_of_x(t, j, n, bank, part, used):
                pair = (j + 2) // 2 % 2
                pe.wait_ge(x3_split, n(0))
                if t is None or t >= 4:
                    pe.wait_ge(used, n(-2))
                product(pair_at(bank), fused_at(0, part), flat(x3_hi[:, pair, :, :, :]),
                        flat(x3_lo[:, pair, :, :, :]), True)

            def recurrent_of_x(t, n, bank, chunk, used):
                if t is None or t >= 0:
                    pe.wait_ge(used, n(1))
                product(pair_at(bank), block_at(chunk), flat(x2_hi), flat(x2_lo), True)

            def gates(t, j, n, pos):
                first_of_pair = j % 2 == 0
                if valid(t, -2) and j == 0:
                    memory_of_x(t, j, n)
                if valid(t):
                    pe.wait_ge(h2_next, n(1))
                    product(step_at(R_ps, j), block_at(R0 + 1), *h2_pair).then_inc(r_sum, 1)
                    product(step_at(Z_ps, j), block_at(Z0 + 1), *h2_pair).then_inc(z_sum, 1)
                if valid(t, -2) and j > 0:
                    memory_of_x(t, j, n)
                if valid(t, -2) and first_of_pair and t != T:
                    fused_of_x(t, j, n, HID_ps, 0, hid_ready)
                if valid(t, 3):
                    if t is None or t > 0:
                        pe.wait_ge(staged2, n(0))
                    if t is None or t >= -2:
                        pe.wait_ge(x2T_ready, n(3))
                    if j == 0 and (t is None or t > 0):
                        pe.wait_ge(p_ready, nth(t, j))
                    x2 = stage[:, (j + 1) % 2, :] if t is None or t > 0 else X[:, (t + 3) * D:(t + 4) * D]
                    transposed(XIN_ps, x2).then_inc(x2_transposed, 1)
                if valid(t, 1) and not first_of_pair:
                    pe.wait_ge(x2_split, n(3))
                    recurrent_of_x(t, n, R_ps, R0, r_ready)
                if valid(t):
                    pe.wait_ge(rh_hi_ready, n(1))
                    high_part(step_at(C_ps, j), block_at(C0 + 1), alone_at(rh_hi))
                    pe.wait_ge(rh_split, n(1))
                    low_part(step_at(C_ps, j), block_at(C0 + 1), alone_at(rh_lo)).then_inc(c_sum, 1)
                if valid(t, -2):
                    pe.wait_ge(h3_hi_ready, n(-1))
                    high_part(step_at(HID_ps, j), fused_at(1, 0), alone_at(h3_hi))
                    pe.wait_ge(h3_split, n(-1))
                    low_part(step_at(HID_ps, j), fused_at(1, 0), alone_at(h3_lo)).then_inc(hid_sum, 1)
                    product(alone_at(M_ps[:, KC * B:]), block_at(MH0), *h3_pair).then_inc(mem_sum, 1)
                    if first_of_pair and t != T:
                        fused_of_x(t, j, n, OUT_ps, 1, out_ready)
                    product(step_at(OUT_ps, j), fused_at(1, 1), *h3_pair).then_inc(out_sum, 1)
                if valid(t, -3):
                    pe.wait_ge(x4_ready, n(-2))
                    if t is None or t >= 4:
                        pe.wait_ge(x4_nat, n(-3))
                    transposed(XOUT_ps, x4T[:, (j + 1) % 2, :]).then_inc(x4_transposed, 1)
                if valid(t, 1) and not first_of_pair:
                    recurrent_of_x(t, n, Z_ps, Z0, z_ready)
                if valid(t) and j == UNROLL - 1 and (t is None or t < T - 1):
                    pe.wait_ge(h2_split_p, nth(t, j))
                    if t is None or t + 3 < T:
                        pe.wait_ge(x2T_ready, n(4))
                    product(alone_at(P_ps), block_at(P0), *h2_pair, True).then_inc(p_sum, 1)
                if valid(t, 1) and not first_of_pair:
                    recurrent_of_x(t, n, C_ps, C0, c_ready)

            known = {}

            def nth(t, j):
                return (t + 1) // UNROLL if t is not None else known["nth" if j else "before"]

            keep_warm(8, XOUT_ps)
            pe.wait_ge(x2_nat, L)
            pe.wait_ge(w_lo_ready, CHUNKS)
            pe.wait_ge(mod_ready, L)
            for t in range(-3, UNROLL):
                gates(t, t % UNROLL, lambda k, t=t: t + k, t)
                if t == -3:
                    keep_warm(8, XOUT_ps)
                if t == 0:
                    keep_warm(20, XOUT_ps)
            with pe.Fori(1, GROUPS - 1) as i:
                base = Count(pe, i * UNROLL)
                known["nth"], known["before"] = pe.snap(i + 1), pe.snap(i)
                for j in range(UNROLL):
                    gates(None, j, lambda k, j=j: base(j + k), i * UNROLL + j)
            for t in range(T - UNROLL, T + 4):
                gates(t, t % UNROLL, lambda k, t=t: t + k, t)
                if t in (T - 1, T):
                    for bank, part, used in ((HID_ps, 0, hid_ready), (OUT_ps, 1, out_ready)):
                        pe.wait_ge(used, t - 1)
                        last_fused_of_x(t - T + 1, bank, part)
                if t in (T, T + 2):
                    keep_warm(14, Z_ps)


_INS = ["x", "cond_1024", "L0_cond_Wx", "L0_cond_Wh", "L0_cond_b", "L1_cond_weight", "L2_cond_Wz", "L2_cond_bz",
        "L2_cond_Wr", "L2_cond_br", "L2_cond_Wh", "L2_cond_bh", "L2_cond_Wp", "L2_cond_bp", "L3_cond_w_W",
        "L3_cond_w_b", "L3_cond_wx_W", "L3_cond_wx_b", "L3_cond_wh_W", "L3_cond_wh_b"]


def kernel(**inputs):
    import numpy as np
    import concourse.bacc as bacc
    from concourse.bass_utils import run_bass_kernel_spmd

    nc = bacc.Bacc("TRN2", target_bir_lowering=False, num_devices=1)
    arrays, aps = {}, {}
    for name in _INS:
        arr = np.ascontiguousarray(inputs[name])
        arrays[f"in_{name}"] = arr
        aps[name] = nc.dram_tensor(f"in_{name}", arr.shape, mybir.dt.from_np(arr.dtype), kind="ExternalInput").ap()
    out = nc.dram_tensor("out_x", arrays["in_x"].shape, F32, kind="ExternalOutput").ap()
    build_kernel(nc, aps, out)
    r = run_bass_kernel_spmd(nc, [arrays], core_ids=[0])
    return r.results[0]["out_x"]
```
